# Optimizing a Trainium2 kernel written in Bass

```python
import numpy as np
import jax
import jax.numpy as jnp

def _softmax(x, axis=-1):
    return jax.nn.softmax(x, axis=axis)

def _gelu(x):
    return jax.nn.gelu(x, approximate=True)

def _silu(x):
    return jax.nn.silu(x)

def _sigmoid(x):
    return jax.nn.sigmoid(x)

def _layernorm(x, axis=-1, eps=1e-05):
    m = jnp.mean(x, axis=axis, keepdims=True)
    v = jnp.var(x, axis=axis, keepdims=True)
    return (x - m) / jnp.sqrt(v + eps)

def _scatter_add(tgt, idx, src, axis=0):
    return tgt.at[idx].add(src)

def _segment_sum(src, seg, n):
    return jax.ops.segment_sum(src, seg, n)
kernel_name = 'mk_vit_tower_cls_d1_tok_img1024_r4_a12e31'

def setup_inputs(seed: int=0):
    np.random.seed(seed)
    _w = jnp.asarray

    def _rec_inputs():
        import jax
        import jax.numpy as jnp
        _rk = jax.random.key(seed)
        x = -0.000356955 + 1 * jax.random.normal(jax.random.fold_in(_rk, 1), (64, 3, 224, 224), jnp.float32)
        cls_tok = 0.02 * jax.random.normal(jax.random.fold_in(_rk, 5), (1, 1, 256), jnp.float32)
        return (x, cls_tok)
    x, cls_tok = _rec_inputs()

    def _L0_tok_setup():
        import jax, jax.numpy as jnp
        import numpy as np
        PATCH = 16
        EMBED = 256
        key = jax.random.key(seed)
        kx, kw = jax.random.split(key, 2)
        x = jax.random.normal(kx, (128, 3, 224, 224), dtype=jnp.float32)
        in_feat = PATCH * PATCH * 3
        W = jax.random.normal(kw, (EMBED, in_feat), dtype=jnp.float32) * 0.02
        b = jnp.zeros((EMBED,), dtype=jnp.float32)
        return {'x': x, 'W': W, 'b': b}
    _L0_tok_all = _L0_tok_setup()
    _L0_tok_in = {k: v for k, v in _L0_tok_all.items() if k in ('W', 'b')}
    del _L0_tok_all

    def _L0_attn_setup():
        import jax, jax.numpy as jnp
        import numpy as np
        N_HEADS = 16
        EPS = 1e-06
        key = jax.random.key(seed)
        ks = jax.random.split(key, 5)
        B, N, D, H = (4, 512, 256, N_HEADS)
        x = jax.random.normal(ks[0], (B, N, D), dtype=jnp.float32)
        Wq = jax.random.normal(ks[1], (D, D), dtype=jnp.float32) * D ** (-0.5)
        Wk = jax.random.normal(ks[2], (D, D), dtype=jnp.float32) * D ** (-0.5)
        Wv = jax.random.normal(ks[3], (D, D), dtype=jnp.float32) * D ** (-0.5)
        Wo = jax.random.normal(ks[4], (D, D), dtype=jnp.float32) * D ** (-0.5)
        q_scale = jnp.ones((H,), dtype=jnp.float32)
        k_scale = jnp.ones((H,), dtype=jnp.float32)
        return {'x': x, 'Wq': Wq, 'Wk': Wk, 'Wv': Wv, 'Wo': Wo, 'q_scale': q_scale, 'k_scale': k_scale}
    _L0_attn_all = _L0_attn_setup()
    _L0_attn_in = {k: v for k, v in _L0_attn_all.items() if k in ('Wq', 'Wk', 'Wv', 'Wo', 'q_scale', 'k_scale')}
    del _L0_attn_all

    def _L0_ffn_setup():
        import jax, jax.numpy as jnp
        import numpy as np
        import math
        BETA = 0.9
        THRESHOLD = 1.0
        NUM_STEPS = 5
        ALPHA = 2.0

        @jax.custom_vjp
        def spike_fn(u):
            return (u > 0).astype(u.dtype)

        def _spike_fwd(u):
            return (spike_fn(u), u)

        def _spike_bwd(u, g):
            s = jnp.pi / 2.0 * ALPHA * u
            return (g * (ALPHA / 2.0) / (1.0 + s * s),)
        spike_fn.defvjp(_spike_fwd, _spike_bwd)
        key = jax.random.key(seed)
        k1, k2, k3 = jax.random.split(key, 3)
        n_embd = 256
        x = jax.random.normal(k1, (4, 512, n_embd), dtype=jnp.float32)
        W_fc = jax.random.normal(k2, (4 * n_embd, n_embd), dtype=jnp.float32) / math.sqrt(n_embd)
        W_proj = jax.random.normal(k3, (n_embd, 4 * n_embd), dtype=jnp.float32) / math.sqrt(4 * n_embd)
        return {'x': x, 'W_fc': W_fc, 'W_proj': W_proj}
    _L0_ffn_all = _L0_ffn_setup()
    _L0_ffn_in = {k: v for k, v in _L0_ffn_all.items() if k in ('W_fc', 'W_proj')}
    del _L0_ffn_all
    return {'x': x, 'cls_tok': cls_tok, 'L0_tok_W': _L0_tok_in['W'], 'L0_tok_b': _L0_tok_in['b'], 'L0_attn_Wq': _L0_attn_in['Wq'], 'L0_attn_Wk': _L0_attn_in['Wk'], 'L0_attn_Wv': _L0_attn_in['Wv'], 'L0_attn_Wo': _L0_attn_in['Wo'], 'L0_attn_q_scale': _L0_attn_in['q_scale'], 'L0_attn_k_scale': _L0_attn_in['k_scale'], 'L0_ffn_W_fc': _L0_ffn_in['W_fc'], 'L0_ffn_W_proj': _L0_ffn_in['W_proj']}

def reference(x, cls_tok, L0_tok_W, L0_tok_b, L0_attn_Wq, L0_attn_Wk, L0_attn_Wv, L0_attn_Wo, L0_attn_q_scale, L0_attn_k_scale, L0_ffn_W_fc, L0_ffn_W_proj):
    import jax
    import jax.numpy as jnp

    def _L0_tok_ref(x, W, b):
        import jax, jax.numpy as jnp
        import numpy as np
        PATCH = 16
        EMBED = 256
        p = PATCH
        B, C, H, Wd = x.shape
        gh, gw = (H // p, Wd // p)
        patches = x.reshape(B, C, gh, p, gw, p).transpose(0, 1, 2, 4, 3, 5)
        patches = patches.reshape(B, gh * gw, p * p * C)
        return jnp.einsum('bnk,ek->bne', patches, W) + b

    def _L0_attn_ref(x, Wq, Wk, Wv, Wo, q_scale, k_scale):
        import jax, jax.numpy as jnp
        import numpy as np
        N_HEADS = 16
        EPS = 1e-06
        B, N, D = x.shape
        H = N_HEADS
        hd = D // H
        q = jax.nn.silu(x @ Wq.T)
        k = jax.nn.silu(x @ Wk.T)
        v = jax.nn.silu(x @ Wv.T)
        q = q.reshape(B, N, H, hd).transpose(0, 2, 1, 3)
        k = k.reshape(B, N, H, hd).transpose(0, 2, 1, 3)
        v = v.reshape(B, N, H, hd).transpose(0, 2, 1, 3)
        r_q = jnp.linalg.norm(q, axis=-1, keepdims=True)
        r_k = jnp.linalg.norm(k, axis=-1, keepdims=True)
        q_dir = q / (r_q + EPS)
        k_dir = k / (r_k + EPS)
        scores = jnp.einsum('bhnd,bhmd->bhnm', q_dir, k_dir)
        sq = q_scale[None, :, None, None]
        sk = k_scale[None, :, None, None]
        scores = scores * (r_q * sq) * (jnp.swapaxes(r_k, -2, -1) * sk)
        mask = jnp.tril(jnp.ones((N, N), dtype=bool))
        scores = jnp.where(mask, scores, -jnp.inf)
        probs = jax.nn.softmax(scores, axis=-1)
        out = jnp.einsum('bhnm,bhmd->bhnd', probs, v)
        out = out.transpose(0, 2, 1, 3).reshape(B, N, D)
        return out @ Wo.T

    def _L0_ffn_ref(x, W_fc, W_proj):
        import jax, jax.numpy as jnp
        import numpy as np
        import math
        BETA = 0.9
        THRESHOLD = 1.0
        NUM_STEPS = 5
        ALPHA = 2.0

        @jax.custom_vjp
        def spike_fn(u):
            return (u > 0).astype(u.dtype)

        def _spike_fwd(u):
            return (spike_fn(u), u)

        def _spike_bwd(u, g):
            s = jnp.pi / 2.0 * ALPHA * u
            return (g * (ALPHA / 2.0) / (1.0 + s * s),)
        spike_fn.defvjp(_spike_fwd, _spike_bwd)
        h = jnp.square(jax.nn.relu(jnp.einsum('bsd,fd->bsf', x, W_fc)))
        y = jnp.einsum('bsf,df->bsd', h, W_proj)

        def step(mem, _):
            reset = jax.lax.stop_gradient(spike_fn(mem - THRESHOLD))
            mem_new = BETA * mem + y - reset * THRESHOLD
            spk = spike_fn(mem_new - THRESHOLD)
            return (mem_new, spk)
        mem0 = jnp.zeros_like(y)
        _, spks = jax.lax.scan(step, mem0, None, length=NUM_STEPS)
        return jnp.sum(spks, axis=0) / NUM_STEPS
    h = _L0_tok_ref(x, L0_tok_W, L0_tok_b)
    h = jnp.concatenate([jnp.broadcast_to(cls_tok, (h.shape[0], 1, h.shape[2])), h], axis=1)
    h = h + _L0_attn_ref(_layernorm(h, axis=-1), L0_attn_Wq, L0_attn_Wk, L0_attn_Wv, L0_attn_Wo, L0_attn_q_scale, L0_attn_k_scale)
    h = h + _L0_ffn_ref(_layernorm(h, axis=-1), L0_ffn_W_fc, L0_ffn_W_proj)
    return h

_drawn_inputs = setup_inputs


def setup_inputs(seed=0):
    import zlib

    import numpy as np

    out = dict(_drawn_inputs(seed))
    spreads = {'L0_tok_b': (0.0, 0.1), 'L0_attn_q_scale': (1.0, 0.2), 'L0_attn_k_scale': (1.0, 0.2)}
    factors = {}
    for name, (base, spread) in spreads.items():
        noise = np.random.default_rng([zlib.crc32(name.encode()), seed]).standard_normal(out[name].shape)
        drawn = base * np.exp(spread * noise) if base else spread * noise
        out[name] = jnp.asarray(drawn.astype(out[name].dtype))
    for name, factor in factors.items():
        out[name] = (out[name] * factor).astype(out[name].dtype)
    return out
```

```python
from contextlib import ExitStack

import numpy as np

import concourse.bass as bass
from concourse import mybir

F32 = mybir.dt.float32
F32R = mybir.dt.float32r
BF16 = mybir.dt.bfloat16
F16 = mybir.dt.float16
I32 = mybir.dt.int32
ALU = mybir.AluOpType
ACT = mybir.ActivationFunctionType
AX = mybir.AxisListType

IMAGES = 64
PAIRS = IMAGES // 2
PATCHES = 196
TOK = PATCHES + 1
T2 = 2 * TOK
D = 256
KIN = 768
HEADS = 16
HD = D // HEADS
FF = 4 * D
P = 128
KC, DC, FC = KIN // P, D // P, FF // P
TAIL = TOK - P
ROWS = (P, TAIL)
VW = 50
NEG = -1e30
LN_EPS = 1e-5
NORM_EPS = 1e-6
RSQRT_SEED = float(0x5F3759DF)
Q_PARTS = (0, 0, 1, 1, 0, 2)
K_PARTS = (0, 1, 0, 1, 2, 0)
KROWS = HD * len(Q_PARTS)
STEPS, BETA, THRESHOLD = 5, 0.9, 1.0

USE_A = {("embed", 0): (0, 0), ("embed", 1): (1, 0), ("turn", 0): (0, 1), ("turn", 1): (1, 1),
         ("back", 0): (0, 2), ("back", 1): (1, 2), ("qk", 0): (0, 3), ("qk", 1): (1, 3),
         ("qk", 2): (0, 4), ("qk", 3): (1, 4), ("norm", 0): (0, 5), ("v", 0): (1, 5), ("v", 1): (0, 6),
         ("v", 2): (1, 6), ("v", 3): (0, 7), ("g", 0): (1, 7), ("g", 1): (0, 8), ("g", 2): (1, 8), ("g", 3): (0, 9)}
N_A = (10, 9)
USE_C = {("wo", 0): (0, 0), ("wo", 1): (1, 0), ("turn", 0): (0, 1), ("turn", 1): (1, 1),
         ("back", 0): (0, 2), ("back", 1): (1, 2), ("ffn2", 0): (0, 7), ("ffn2", 1): (1, 7)}
USE_C.update({("ffn1", f): (f % 2, 3 + f // 2) for f in range(FC)})
N_C = (8, 8)
N_S = 2 * (HEADS + 1)
N_ST = 2 * HEADS


def spike_thresholds():
    f = np.float32

    def count(y):
        mem, n = f(0), 0
        for _ in range(STEPS):
            mem = f(f(f(BETA) * mem) + y) - f(mem - f(THRESHOLD) > 0)
            n += int(mem - f(THRESHOLD) > 0)
        return n

    out = []
    for want in range(1, STEPS + 1):
        lo, hi = int(f(0.01).view(np.int32)), int(f(2.0).view(np.int32))
        while hi - lo > 1:
            mid = (lo + hi) // 2
            if count(np.int32(mid).view(np.float32)) >= want:
                hi = mid
            else:
                lo = mid
        out.append(float(np.int32(lo).view(np.float32)))
    return out


def attention_head(s, behind):
    n = s - 4 - behind
    lag = 0
    if n < 0:
        n, lag = n + 2 * HEADS, -1
    return (1, lag - 1, n) if n < HEADS else (0, lag, n - HEADS)


def order():
    fill = {s: [] for s in range(2 * HEADS)}

    def put(slot, step, k, lag):
        fill[slot].append((step, k, lag))

    put(0, "embed_mm", 0, 1)
    put(3, "embed_out", 0, 1)
    put(3, "embed_mm", 1, 1)
    put(6, "embed_out", 1, 1)
    put(7, "turn1_mm", 0, 1)
    put(7, "turn1_mm", 1, 1)
    put(8, "stats1", 0, 1)
    put(8, "rstd1", 0, 1)
    put(10, "apply1", 0, 1)
    put(10, "back1_mm", 0, 1)
    put(10, "back1_mm", 1, 1)
    put(11, "back1_out", 0, 1)
    put(11, "back1_out", 1, 1)
    for c in range(4):
        put(11 + c, "qk_mm", c, 1)
        put(12 + c, "silu_qk", c, 1)
        put(13 + c, "square", c, 1)
    put(16, "norm_mm", 0, 1)
    put(17, "norm_out", 0, 1)
    for t in range(4):
        put(17 + t // 2, "v_mm", t, 1)
        put(18 + t // 2, "silu_v", t, 1)
        put(22 + t // 2, "split_v", t, 1)
    put(23, "gate", 0, 1)
    for c in range(4):
        put(24 + c // 2, "g_mm", c, 1)
        put(25 + c // 2, "q_hat", c, 1)
        put(26 + c // 2, "split_q", c, 1)
    put(28, "restack", 0, 1)

    for f in range(FC):
        put(5 + f + (f > 3), "ffn1_mm", f, -2)
        put(6 + f + (f > 3), "ffn1_out", f, -2)
    put(16, "ffn2_mm", 0, -2)
    put(20, "ffn2_mm", 1, -2)
    put(22, "spikes", 0, -2)
    put(8, "ot_mm", 0, -1)
    put(9, "ot_out", 0, -1)
    put(25, "ot_mm", 1, -1)
    put(26, "ot_out", 1, -1)
    put(27, "wo_mm", 0, -1)
    put(27, "wo_mm", 1, -1)
    put(28, "wo_out", 0, -1)
    put(28, "wo_out", 1, -1)
    put(29, "turn2_mm", 0, -1)
    put(29, "turn2_mm", 1, -1)
    put(30, "stats2", 0, -1)
    put(30, "rstd2", 0, -1)
    put(31, "apply2", 0, -1)
    put(31, "back2_mm", 0, -1)
    put(31, "back2_mm", 1, -1)
    put(1, "back2_out", 0, -2)
    put(1, "back2_out", 1, -2)
    put(29, "keep_h", 0, 0)

    out = []
    for s in range(2 * HEADS):
        if s == 0:
            out += [("max_mm", 1, -1), ("max_out", 1, -1)]
        if s == HEADS:
            out += [("max_mm", 0, 0), ("max_out", 0, 0)]
        out.append(("score", s, 0))
        for step, behind in (("st", 0), ("p", 1), ("pv", 2), ("o", 3)):
            img, lag, h = attention_head(s, behind)
            out.append((step, img * HEADS + h, lag))
        out += fill[s]
    return out


ORDER = order()
LOOP_FROM = 3


def program(nc, x_t, w_tok, b_tok, cls, w_qk, w_v, w_o, w_fc, w_proj, q_scale, k_scale,
            eye, row_mask, key_mask, head_rows, head_cols, out_t):
    thresholds = spike_thresholds()
    with ExitStack() as ctx:
        def sb(name, shape, dt=F32):
            return ctx.enter_context(nc.sbuf_tensor(name, shape, dt))

        def psum(name):
            return ctx.enter_context(nc.psum_tensor(name, [P, 512], F32))

        def sem(name):
            return ctx.enter_context(nc.semaphore(name))

        wtok = sb("wtok", [P, KC, D])
        btok = sb("btok", [P, DC])
        clsT = sb("clsT", [P, DC])
        wqk = sb("wqk", [P, DC, 2 * D])
        wv = sb("wv", [P, DC, D])
        wo = sb("wo", [P, DC, D])
        wfc = sb("wfc", [P, DC, FF])
        wproj = sb("wproj", [P, FC, D])
        qsc = sb("qsc", [P, DC])
        ksc = sb("ksc", [P, DC])
        sc = sb("sc", [P, 4])
        eyef = sb("eyef", [P, P])
        eyeb = sb("eyeb", [P, P], BF16)
        rowmask = sb("rowmask", [P, P + TOK])
        keymask = sb("keymask", [P, P], BF16)
        hrows = sb("hrows", [P, 4, P], F32R)
        hcols = sb("hcols", [2 * HEADS, 4, P], F32R)

        x_sb = sb("x_sb", [P, KC, 2 * PATCHES])
        hA = [sb(f"hA{b}", [P, DC, 2, TOK]) for b in range(2)]
        hC = sb("hC", [P, DC, T2])
        st1 = sb("st1", [P, 4, 6])
        mv1 = sb("mv1", [P, 4, 2])
        nw1 = sb("nw1", [P, 3, 4])
        nt = sb("nt", [P, 4, D])
        lnT = sb("lnT", [P, DC, T2])
        th = sb("th", [P, 4, T2])
        s2 = sb("s2", [P, 4, T2])
        sq = sb("sq", [P, 4, T2], F32R)
        r2 = sb("r2", [2 * HEADS, T2])
        nwr = sb("nwr", [2 * HEADS, 2, T2])
        g_sb = sb("g_sb", [2 * HEADS, T2], F32R)
        parts = [sb(f"part{j}", [P, 4, T2], BF16) for j in range(3)]
        tv = sb("tv", [P, 4, D])
        v2 = sb("v2", [P, 4, D])
        qst = [sb(f"qst{b}", [KROWS + 3, HEADS, T2], BF16) for b in range(2)]
        kst = [sb(f"kst{b}", [KROWS + 3, HEADS * T2 + 64], BF16) for b in range(2)]
        vst = [sb(f"vst{b}", [P, 4, HEADS, VW], BF16) for b in range(2)]
        mx = sb("mx", [P, 2, 2, HEADS])
        mr = sb("mr", [HEADS, TOK])
        mp = sb("mp", [HEADS, 3, TOK], BF16)
        p32 = sb("p32", [P, 2, TOK + TAIL])
        p1 = sb("p1", [P, 2, TOK + TAIL], F16)
        p2 = sb("p2", [P, 2, TOK + TAIL], F16)
        rd = sb("rd", [P, 4, HEADS])
        ot = sb("ot", [P, 4, HEADS, HD])
        oT = sb("oT", [P, DC, 2, TOK])
        h1 = sb("h1", [P, DC, T2])
        st2 = sb("st2", [P, 4, 6])
        mv2 = sb("mv2", [P, 4, 2])
        nw2 = sb("nw2", [P, 3, 4])
        l2T = sb("l2T", [P, DC, T2])
        rr = sb("rr", [P, 2, T2])
        hs = sb("hs", [P, FC, T2])
        cn = sb("cn", [P, DC, T2])
        hrowsf = hs[:, 0:4, 0:P]
        hcolsf = hs[0:2 * HEADS, 4:8, 0:P]
        keymaskf = hs[:, 0, P:2 * P]

        bankA = [psum("bankA0"), psum("bankA1")]
        bankC = [psum("bankC0"), psum("bankC1")]
        bankS, bankST, bankO, bankX = psum("bankS"), psum("bankST"), psum("bankO"), psum("bankX")

        fullA, freeA = [sem("fullA0"), sem("fullA1")], [sem("freeA0"), sem("freeA1")]
        fullC, freeC = [sem("fullC0"), sem("fullC1")], [sem("freeC0"), sem("freeC1")]
        fullS, freeS = sem("fullS"), sem("freeS")
        fullST, freeST = sem("fullST"), sem("freeST")
        freeO = sem("freeO")
        fullX, freeX = sem("fullX"), sem("freeX")
        s_w = sem("weights_in")
        s_const = sem("constants_ready")
        s_x = sem("x_in")
        s_hc = sem("h_kept")
        s_bn1, s_ag1, s_ln1 = sem("bn_stats_1"), sem("bn_aggr_1"), sem("rstd_1_steps")
        s_bn2, s_ag2, s_ln2 = sem("bn_stats_2"), sem("bn_aggr_2"), sem("rstd_2_steps")
        s_th, s_sq = sem("tanh_qk"), sem("squares")
        s_rn, s_rec = sem("norm_steps"), sem("norm_reciprocal")
        s_q1, s_r1, s_q2, s_q3 = sem("qk_part1"), sem("qk_rest"), sem("qk_part2"), sem("qk_part3")
        s_tv, s_v1, s_rv, s_v2, s_v3 = sem("tanh_v"), sem("v_part1"), sem("v_rest"), sem("v_part2"), sem("v_part3")
        s_stack = sem("stack_in")
        s_m1, s_m2, s_m3, s_mrow = sem("max_part1"), sem("max_part2"), sem("max_part3"), sem("max_rows_in")
        s_p1, s_p2, s_pv = sem("p_part1"), sem("p_part2"), sem("pv_done")
        s_ot = sem("heads_divided")
        s_hs = sem("ffn_hidden")
        s_cn, s_ow, s_out = sem("count_steps"), sem("out_ready"), sem("out_stored")

        block = ctx.enter_context(nc.Block())

        def due(count):
            return not isinstance(count, int) or count > 0

        def run(eng, mine):
            def peeled(i):
                for step, k, lag in ORDER:
                    if step in mine and 0 <= i + lag < PAIRS:
                        mine[step](i + lag, (i + lag) % 2, k)

            for i in range(-1, LOOP_FROM):
                peeled(i)
            with eng.Fori(LOOP_FROM, PAIRS - 2, 2) as i:
                for u in range(2):
                    for step, k, lag in ORDER:
                        if step in mine:
                            mine[step](i + (u + lag), (LOOP_FROM + u + lag) % 2, k)
            for i in range(PAIRS - 1, PAIRS + 2):
                peeled(i)

        @block.sync
        def _(sp):
            loads = [(wtok[:, :, :], w_tok), (btok[:, :], b_tok), (clsT[:, :], cls), (eyef[:, :], eye),
                     (wqk[:, :, :], w_qk), (wv[:, :, :], w_v), (hrowsf, head_rows), (hcolsf, head_cols),
                     (qsc[:, :], q_scale), (ksc[:, :], k_scale), (rowmask[:, :], row_mask),
                     (keymaskf, key_mask), (wo[:, :, :], w_o), (wfc[:, :, :], w_fc), (wproj[:, :, :], w_proj)]
            for dst, src in loads:
                sp.dma_start(dst, src).then_inc(s_w, 16)

            def load_x(p, b, k):
                if due(N_A[1] * (p - 1) + 1):
                    sp.wait_ge(fullA[1], N_A[1] * (p - 1) + 1)
                sp.dma_start(x_sb[:, :, :], x_t[p].rearrange("p (k n) -> p k n", k=KC)).then_inc(s_x, 16)

            def keep_h(p, b, k):
                sp.wait_ge(freeA[0], N_A[0] * p + 1)
                sp.wait_ge(freeA[1], N_A[1] * p + 1)
                if due(N_C[0] * (p - 1) + 1):
                    sp.wait_ge(freeC[0], N_C[0] * (p - 1) + 1)
                if due(N_C[1] * (p - 1) + 1):
                    sp.wait_ge(freeC[1], N_C[1] * (p - 1) + 1)
                sp.dma_start(hC[:, :, :], hA[b][:, :, :, :].rearrange("p c i n -> p c (i n)")).then_inc(s_hc, 16)

            def restack(p, b, k):
                if due(N_ST * (p - 1)):
                    sp.wait_ge(fullST, N_ST * (p - 1))
                sp.wait_ge(s_q1, 4 * (p + 1))
                sp.wait_ge(s_q2, 4 * (p + 1))
                sp.wait_ge(s_q3, 4 * (p + 1))
                for c in range(DC):
                    for j in range(len(Q_PARTS)):
                        rows = slice(HD * j, HD * (j + 1))
                        heads = slice(8 * c, 8 * (c + 1))
                        sp.dma_start(qst[b][rows, heads, :], parts[Q_PARTS[j]][:, c, :]).then_inc(s_stack, 16)
                        kview = kst[b][rows, 8 * c * T2:8 * (c + 1) * T2].rearrange("d (h n) -> d h n", h=8)
                        sp.dma_start(kview, parts[K_PARTS[j]][:, 2 + c, :]).then_inc(s_stack, 16)

            def max_rows(p, b, img):
                sp.wait_ge(s_m3, 2 * p + img + 1)
                for j in range(3):
                    sp.dma_start(qst[b][KROWS + j:KROWS + j + 1, :, img * TOK:(img + 1) * TOK],
                                 mp[:, j, :]).then_inc(s_mrow, 16)

            def store(p, b, k):
                sp.wait_ge(s_ow, 2 * (p + 1))
                sp.dma_start(out_t[p].rearrange("p (c n) -> p c n", c=DC), cn[:, :, :]).then_inc(s_out, 16)

            run(sp, {"embed_mm": lambda p, b, k: load_x(p, b, k) if k == 0 else None,
                     "keep_h": keep_h, "restack": restack, "max_out": max_rows, "spikes": store})
            sp.wait_ge(s_out, 16 * PAIRS)

        @block.tensor
        def _(pe):
            pe.wait_ge(s_const, 1)
            pe.wait_ge(s_w, 16 * 15)

            def embed(p, b, m):
                bank, use = USE_A["embed", m]
                pe.wait_ge(s_x, 16 * (p + 1))
                if due(N_A[bank] * p + use):
                    pe.wait_ge(freeA[bank], N_A[bank] * p + use)
                for k in range(KC):
                    mm = pe.matmul(bankA[bank][:, 0:2 * PATCHES], wtok[:, k, m * P:(m + 1) * P], x_sb[:, k, :],
                                   start=(k == 0), stop=(k == KC - 1))
                mm.then_inc(fullA[bank], 1)

            def turn(p, img, src, banks, full, free, per, uses):
                bank, use = uses["turn", img]
                pe.wait_ge(free[0], per[0] * p + 1)
                pe.wait_ge(free[1], per[1] * p + 1)
                for c in range(2):
                    for m in range(DC):
                        n0 = c * P
                        mm = pe.transpose(banks[bank][0:ROWS[c], c * D + m * P:c * D + (m + 1) * P],
                                          src(m, img, n0, n0 + ROWS[c]), eyef[:, :])
                mm.then_inc(full[bank], 1)

            def back(p, m, src, banks, full, free, per, uses):
                bank, use = uses["back", m]
                pe.wait_ge(free[0], per[0] * p + 2)
                pe.wait_ge(free[1], per[1] * p + 2)
                for t in range(4):
                    n0 = (t // 2) * TOK + (t % 2) * P
                    r = ROWS[t % 2]
                    mm = pe.transpose(banks[bank][:, n0:n0 + r], src[0:r, t, m * P:(m + 1) * P], eyef[0:r, 0:r])
                mm.then_inc(full[bank], 1)

            def qk(p, b, c):
                bank, use = USE_A["qk", c]
                pe.wait_ge(freeA[1 - bank], N_A[1 - bank] * p + 3)
                if due(N_A[bank] * p + use):
                    pe.wait_ge(freeA[bank], N_A[bank] * p + use)
                for k in range(DC):
                    mm = pe.matmul(bankA[bank][:, 0:T2], wqk[:, k, c * P:(c + 1) * P], lnT[:, k, :],
                                   start=(k == 0), stop=(k == DC - 1))
                mm.then_inc(fullA[bank], 1)

            def v(p, b, t):
                bank, use = USE_A["v", t]
                n0, r = (t // 2) * TOK + (t % 2) * P, ROWS[t % 2]
                if due(N_A[bank] * p + use):
                    pe.wait_ge(freeA[bank], N_A[bank] * p + use)
                for k in range(DC):
                    mm = pe.matmul(bankA[bank][0:r, 0:D], lnT[:, k, n0:n0 + r], wv[:, k, :],
                                   start=(k == 0), stop=(k == DC - 1))
                mm.then_inc(fullA[bank], 1)

            def norm(p, b, _k):
                bank, use = USE_A["norm", 0]
                pe.wait_ge(s_sq, 4 * (p + 1))
                if due(N_A[bank] * p + use):
                    pe.wait_ge(freeA[bank], N_A[bank] * p + use)
                for c in range(4):
                    mm = pe.matmul(bankA[bank][:, 0:T2], hrows[:, c, :], sq[:, c, :], start=(c == 0), stop=(c == 3))
                mm.then_inc(fullA[bank], 1)

            def g(p, b, c):
                bank, use = USE_A["g", c]
                pe.wait_ge(s_rn, 16 * (p + 1))
                if due(N_A[bank] * p + use):
                    pe.wait_ge(freeA[bank], N_A[bank] * p + use)
                pe.matmul(bankA[bank][:, 0:T2], hcols[:, c, :], g_sb[:, :], start=True,
                          stop=True).then_inc(fullA[bank], 1)

            def score(p, b, s):
                img, h = s // HEADS, s % HEADS
                if s == 0:
                    pe.wait_ge(s_stack, 16 * 24 * (p + 1))
                if due(N_S * p + img * (HEADS + 1) + h):
                    pe.wait_ge(freeS, N_S * p + img * (HEADS + 1) + h)
                q0, k0 = img * TOK, h * T2 + img * TOK
                pe.matmul(bankS[:, 0:P], qst[b][0:KROWS, h, q0:q0 + P], kst[b][0:KROWS, k0:k0 + P],
                          start=True, stop=True)
                pe.matmul(bankS[0:TAIL, P:P + TOK], qst[b][0:KROWS, h, q0 + P:q0 + TOK],
                          kst[b][0:KROWS, k0:k0 + TOK], start=True, stop=True).then_inc(fullS, 1)

            def max_turn(p, b, img):
                use = N_S * p + img * (HEADS + 1) + HEADS
                if due(use):
                    pe.wait_ge(freeS, use)
                pe.transpose(bankS[0:HEADS, 0:P], mx[:, img, 0, :], eyef[:, :])
                pe.transpose(bankS[0:HEADS, P:TOK], mx[0:TAIL, img, 1, :], eyef[0:TAIL, 0:TAIL]).then_inc(fullS, 1)

            def st(p, b, n):
                img, h = n // HEADS, n % HEADS
                if h == 0:
                    if due(16 * 3 * (2 * p + img + 1)):
                        pe.wait_ge(s_mrow, 16 * 3 * (2 * p + img + 1))
                if due(N_ST * p + n):
                    pe.wait_ge(freeST, N_ST * p + n)
                q0, k0 = img * TOK, h * T2 + img * TOK
                pe.matmul(bankST[:, 0:TOK], kst[b][:, k0:k0 + P], qst[b][:, h, q0:q0 + TOK], start=True, stop=False,
                          skip_group_check=True)
                pe.matmul(bankST[:, 0:P], eyeb[:, :], keymask[:, :], start=False, stop=True, skip_group_check=True)
                pe.matmul(bankST[:, TOK:TOK + TAIL], kst[b][:, k0 + P:k0 + 2 * P], qst[b][:, h, q0 + P:q0 + TOK],
                          start=True, stop=False, skip_group_check=True)
                pe.matmul(bankST[:, TOK:TOK + TAIL], eyeb[:, :], keymask[:, 0:TAIL], start=False, stop=True,
                          skip_group_check=True).then_inc(fullST, 1)

            def pv(p, b, n):
                img, h = n // HEADS, n % HEADS
                if n == 0:
                    pe.wait_ge(s_v2, 4 * (p + 1))
                    pe.wait_ge(s_v3, 4 * (p + 1))
                pe.wait_ge(s_p2, N_ST * p + n + 1)
                if n % 4 == 0:
                    if due(8 * p + n // 4):
                        pe.wait_ge(freeO, 8 * p + n // 4)
                w, hh, t = n % 2, h % 4, 2 * img
                o0 = bankO[:, hh * VW:(hh + 1) * VW]
                o1 = bankO[0:TAIL, (4 + hh) * VW:(5 + hh) * VW]
                pe.matmul(o0, p1[:, w, 0:P], vst[b][:, t, h, :], start=True, stop=False, skip_group_check=True)
                pe.matmul(o0, p2[:, w, 0:P], vst[b][:, t, h, :], start=False, stop=True, skip_group_check=True)
                pe.matmul(o1, p1[:, w, P:TOK], vst[b][:, t, h, :], start=True, stop=False, skip_group_check=True)
                pe.matmul(o1, p2[:, w, P:TOK], vst[b][:, t, h, :], start=False, stop=False, skip_group_check=True)
                pe.matmul(o1, p1[0:TAIL, w, TOK:], vst[b][0:TAIL, t + 1, h, :], start=False, stop=False,
                          skip_group_check=True)
                pe.matmul(o1, p2[0:TAIL, w, TOK:], vst[b][0:TAIL, t + 1, h, :], start=False, stop=True,
                          skip_group_check=True).then_inc(s_pv, 1)

            def ot_turn(p, b, img):
                pe.wait_ge(s_ot, 8 * p + 4 * (img + 1))
                if due(2 * p + img):
                    pe.wait_ge(freeX, 2 * p + img)
                for m in range(DC):
                    for c in range(2):
                        r = ROWS[c]
                        mm = pe.transpose(bankX[:, m * TOK + c * P:m * TOK + c * P + r],
                                          ot[0:r, 2 * img + c, 8 * m:8 * (m + 1), :].rearrange("p h d -> p (h d)"),
                                          eyef[0:r, 0:r])
                mm.then_inc(fullX, 1)

            def project(p, b, m):
                bank, use = USE_C["wo", m]
                pe.wait_ge(freeX, 2 * (p + 1))
                if due(N_C[bank] * p + use):
                    pe.wait_ge(freeC[bank], N_C[bank] * p + use)
                for k in range(DC):
                    mm = pe.matmul(bankC[bank][:, 0:T2], wo[:, k, m * P:(m + 1) * P],
                                   oT[:, k, :, :].rearrange("p i n -> p (i n)"), start=(k == 0), stop=(k == DC - 1))
                mm.then_inc(fullC[bank], 1)

            def ffn1(p, b, f):
                bank, use = USE_C["ffn1", f]
                pe.wait_ge(freeC[1 - bank], N_C[1 - bank] * p + 3)
                if due(N_C[bank] * p + use):
                    pe.wait_ge(freeC[bank], N_C[bank] * p + use)
                for k in range(DC):
                    mm = pe.matmul(bankC[bank][:, 0:T2], wfc[:, k, f * P:(f + 1) * P], l2T[:, k, :],
                                   start=(k == 0), stop=(k == DC - 1))
                mm.then_inc(fullC[bank], 1)

            def ffn2(p, b, m):
                bank, use = USE_C["ffn2", m]
                pe.wait_ge(s_hs, FC * (p + 1))
                if due(N_C[bank] * p + use):
                    pe.wait_ge(freeC[bank], N_C[bank] * p + use)
                for f in range(FC):
                    mm = pe.matmul(bankC[bank][:, 0:T2], wproj[:, f, m * P:(m + 1) * P], hs[:, f, :],
                                   start=(f == 0), stop=(f == FC - 1))
                mm.then_inc(fullC[bank], 1)

            run(pe, {
                "embed_mm": embed,
                "turn1_mm": lambda p, b, k: turn(p, k, lambda m, i, a, e: hA[b][:, m, i, a:e],
                                                 bankA, fullA, freeA, N_A, USE_A),
                "back1_mm": lambda p, b, k: back(p, k, nt, bankA, fullA, freeA, N_A, USE_A),
                "qk_mm": qk, "v_mm": v, "norm_mm": norm, "g_mm": g,
                "score": score, "max_mm": max_turn, "st": st, "pv": pv, "ot_mm": ot_turn, "wo_mm": project,
                "turn2_mm": lambda p, b, k: turn(p, k, lambda m, i, a, e: h1[:, m, i * TOK + a:i * TOK + e],
                                                 bankC, fullC, freeC, N_C, USE_C),
                "back2_mm": lambda p, b, k: back(p, k, nt, bankC, fullC, freeC, N_C, USE_C),
                "ffn1_mm": ffn1, "ffn2_mm": ffn2})

        @block.scalar
        def _(act):
            act.wait_ge(s_w, 16 * 15)
            act.wait_ge(s_const, 1)

            def embed_out(p, b, m):
                bank, use = USE_A["embed", m]
                if due(16 * (p - 1)):
                    act.wait_ge(s_hc, 16 * (p - 1))
                act.wait_ge(fullA[bank], N_A[bank] * p + use + 1)
                act.activation(hA[b][:, m, :, 1:TOK], bankA[bank][:, 0:2 * PATCHES].rearrange("p (i n) -> p i n", i=2),
                               ACT.Identity, bias=btok[:, m:m + 1]).then_inc(freeA[bank], 1)

            def back_out(p, m, dst, banks, full, free, per, uses):
                bank, use = uses["back", m]
                act.wait_ge(full[bank], per[bank] * p + use + 1)
                act.activation(dst[:, m, :], banks[bank][:, 0:T2], ACT.Copy).then_inc(free[bank], 1)

            def tanh_qk(p, b, c):
                bank, use = USE_A["qk", c]
                if due(4 * p):
                    act.wait_ge(s_q3, 4 * p)
                act.wait_ge(fullA[bank], N_A[bank] * p + use + 1)
                act.activation(th[:, c, :], bankA[bank][:, 0:T2], ACT.Tanh, scale=0.5).then_inc(s_th, 1)

            def square(p, b, c):
                bank, use = USE_A["qk", c]
                act.wait_ge(freeA[bank], N_A[bank] * p + use + 1)
                act.activation(sq[:, c, :], s2[:, c, :], ACT.Square, scale=0.5).then_inc(s_sq, 1)

            def norm_out(p, b, k):
                bank, use = USE_A["norm", 0]
                if due(16 * p):
                    act.wait_ge(s_rn, 16 * p)
                act.wait_ge(fullA[bank], N_A[bank] * p + use + 1)
                act.activation(r2[:, :], bankA[bank][0:2 * HEADS, 0:T2], ACT.Copy).then_inc(freeA[bank], 1)

            def tanh_v(p, b, t):
                bank, use = USE_A["v", t]
                r = ROWS[t % 2]
                if due(4 * p):
                    act.wait_ge(s_v3, 4 * p)
                act.wait_ge(fullA[bank], N_A[bank] * p + use + 1)
                act.activation(tv[0:r, t, :], bankA[bank][0:r, 0:D], ACT.Tanh, scale=0.5).then_inc(s_tv, 1)

            def split_v(p, b, t):
                bank, use = USE_A["v", t]
                r = ROWS[t % 2]
                heads = lambda a: a[0:r, t, :].rearrange("p (h d) -> p h d", h=HEADS)
                if due(N_ST * (p - 1)):
                    act.wait_ge(s_pv, N_ST * (p - 1))
                act.wait_ge(freeA[bank], N_A[bank] * p + use + 1)
                act.activation(vst[b][0:r, t, :, 0:HD], heads(v2), ACT.Copy).then_inc(s_v1, 1)
                act.wait_ge(s_rv, 4 * p + t + 1)
                act.activation(vst[b][0:r, t, :, HD:2 * HD], heads(tv), ACT.Copy).then_inc(s_v2, 1)

            def split_q(p, b, c):
                bank, use = USE_A["g", c]
                if due(16 * 24 * p):
                    act.wait_ge(s_stack, 16 * 24 * p)
                act.wait_ge(freeA[bank], N_A[bank] * p + use + 1)
                act.activation(parts[0][:, c, :], th[:, c, :], ACT.Copy, scale=sc[:, c:c + 1]).then_inc(s_q1, 1)
                act.wait_ge(s_r1, 4 * p + c + 1)
                act.activation(parts[1][:, c, :], th[:, c, :], ACT.Copy).then_inc(s_q2, 1)

            def max_out(p, b, img):
                if due(16 * 3 * (2 * p + img)):
                    act.wait_ge(s_mrow, 16 * 3 * (2 * p + img))
                act.wait_ge(fullS, N_S * p + img * (HEADS + 1) + HEADS + 1)
                act.activation(mp[:, 0, :], bankS[0:HEADS, 0:TOK], ACT.Copy).then_inc(s_m1, 1)
                act.wait_ge(freeS, N_S * p + (img + 1) * (HEADS + 1))
                act.activation(mp[:, 1, :], mr[:, :], ACT.Copy).then_inc(s_m2, 1)

            def exp(p, b, n):
                if due(N_ST * p + n - 1):
                    act.wait_ge(s_p2, N_ST * p + n - 1)
                act.wait_ge(fullST, N_ST * p + n + 1)
                act.activation(p32[:, n % 2, :], bankST[:, 0:TOK + TAIL], ACT.Exp).then_inc(freeST, 1)

            def part1(p, b, n):
                if due(N_ST * p + n - 1):
                    act.wait_ge(s_pv, N_ST * p + n - 1)
                act.wait_ge(freeST, N_ST * p + n + 1)
                act.activation(p1[:, n % 2, :], p32[:, n % 2, :], ACT.Copy).then_inc(s_p1, 1)

            def ot_out(p, b, img):
                act.wait_ge(fullX, 2 * p + img + 1)
                act.activation(oT[:, :, img, :], bankX[:, 0:2 * TOK].rearrange("p (m n) -> p m n", m=DC),
                               ACT.Copy).then_inc(freeX, 1)

            def relu(p, b, f):
                bank, use = USE_C["ffn1", f]
                if due(FC * p + f - 1):
                    act.wait_ge(s_hs, FC * p + f - 1)
                act.wait_ge(fullC[bank], N_C[bank] * p + use + 1)
                act.activation(rr[:, f % 2, :], bankC[bank][:, 0:T2], ACT.Relu).then_inc(freeC[bank], 1)

            run(act, {
                "embed_out": embed_out,
                "back1_out": lambda p, b, k: back_out(p, k, lnT, bankA, fullA, freeA, N_A, USE_A),
                "silu_qk": tanh_qk, "square": square, "norm_out": norm_out, "silu_v": tanh_v, "split_v": split_v,
                "split_q": split_q, "max_out": max_out, "st": exp, "p": part1, "ot_out": ot_out,
                "back2_out": lambda p, b, k: back_out(p, k, l2T, bankC, fullC, freeC, N_C, USE_C),
                "ffn1_out": relu})

        @block.vector
        def _(dve):
            dve.wait_ge(s_w, 16 * 15)
            for b in range(2):
                dve.memset(kst[b][:, HEADS * T2:], 0.0)
                dve.memset(kst[b][KROWS:KROWS + 3, 0:HEADS * T2], -1.0)
                dve.memset(vst[b][:, :, :, 3 * HD:3 * HD + 1], 2.0)
                dve.memset(vst[b][:, :, :, 3 * HD + 1:], 0.0)
            dve.memset(mv1[:, :, :], 1.0)
            dve.memset(mv2[:, :, :], 1.0)
            dve.tensor_copy(eyeb[:, :], eyef[:, :])
            dve.tensor_copy(keymask[:, :], keymaskf)
            dve.tensor_copy(hrows[:, :, :], hrowsf)
            dve.tensor_copy(hcols[:, :, :], hcolsf)
            for b in range(2):
                for img in range(2):
                    dve.tensor_copy(hA[b][:, :, img, 0], clsT[:, :])
            dve.memset(sc[:, 2:4], 1.0)
            dve.scalar_tensor_tensor(out=sc[:, 0:2], in0=qsc[:, :], scalar=0.25, in1=ksc[:, :],
                                     op0=ALU.mult, op1=ALU.mult).then_inc(s_const, 1)

            def stats(p, banks, full, per, st, mv, s_bn, s_ag):
                for t in range(4):
                    img, r = t // 2, ROWS[t % 2]
                    dve.wait_ge(full[img], per[img] * p + 2)
                    dve.bn_stats(st[0:r, t, :], banks[img][0:r, (t % 2) * D:(t % 2 + 1) * D]).then_inc(s_bn, 1)
                for t in range(4):
                    r = ROWS[t % 2]
                    dve.wait_ge(s_bn, 4 * p + t + 1)
                    dve.nop(nofuse=True)
                    dve.bn_aggr(mv[0:r, t, :], st[0:r, t, :]).then_inc(s_ag, 1)

            def apply(p, banks, free, mv, nw, dst, s_ln):
                dve.wait_ge(s_ln, 14 * (p + 1))
                for t in range(4):
                    img, r = t // 2, ROWS[t % 2]
                    ins = dve.tensor_scalar(dst[0:r, t, :], banks[img][0:r, (t % 2) * D:(t % 2 + 1) * D],
                                            mv[0:r, t, 0:1], nw[0:r, 1, t:t + 1], ALU.subtract, ALU.mult)
                    if t % 2:
                        ins.then_inc(free[img], 1)

            def silu_qk(p, b, c):
                bank, use = USE_A["qk", c]
                dve.wait_ge(s_th, 4 * p + c + 1)
                dve.scalar_tensor_tensor(out=s2[:, c, :], in0=th[:, c, :], scalar=1.0, in1=bankA[bank][:, 0:T2],
                                         op0=ALU.add, op1=ALU.mult).then_inc(freeA[bank], 1)

            def silu_v(p, b, t):
                bank, use = USE_A["v", t]
                r = ROWS[t % 2]
                dve.wait_ge(s_tv, 4 * p + t + 1)
                dve.scalar_tensor_tensor(out=v2[0:r, t, :], in0=tv[0:r, t, :], scalar=1.0, in1=bankA[bank][0:r, 0:D],
                                         op0=ALU.add, op1=ALU.mult).then_inc(freeA[bank], 1)

            def split_v(p, b, t):
                r = ROWS[t % 2]
                dve.wait_ge(s_v1, 4 * p + t + 1)
                dve.tensor_tensor(tv[0:r, t, :].rearrange("p (h d) -> p h d", h=HEADS),
                                  v2[0:r, t, :].rearrange("p (h d) -> p h d", h=HEADS),
                                  vst[b][0:r, t, :, 0:HD], ALU.subtract).then_inc(s_rv, 1)

            def gate(p, b, k):
                dve.wait_ge(s_rn, 16 * p + 15)
                dve.reciprocal(r2[:, :], nwr[:, 1, :]).then_inc(s_rec, 1)

            def q_hat(p, b, c):
                bank, use = USE_A["g", c]
                dve.wait_ge(fullA[bank], N_A[bank] * p + use + 1)
                dve.scalar_tensor_tensor(out=th[:, c, :], in0=bankA[bank][:, 0:T2], scalar=1.0, in1=s2[:, c, :],
                                         op0=ALU.subtract, op1=ALU.mult).then_inc(freeA[bank], 1)

            def split_q(p, b, c):
                dve.wait_ge(s_q1, 4 * p + c + 1)
                dve.scalar_tensor_tensor(out=th[:, c, :], in0=th[:, c, :], scalar=sc[:, c:c + 1],
                                         in1=parts[0][:, c, :], op0=ALU.mult, op1=ALU.subtract).then_inc(s_r1, 1)

            def score_max(p, b, s):
                img, h = s // HEADS, s % HEADS
                dve.wait_ge(fullS, N_S * p + img * (HEADS + 1) + h + 1)
                dve.nop(nofuse=True)
                dve.tensor_tensor_reduce(out=bankS[:, 0:P], in0=bankS[:, 0:P], in1=rowmask[:, 0:P], scale=1.0,
                                         scalar=2 * NEG, op0=ALU.add, op1=ALU.max, accum_out=mx[:, img, 0, h:h + 1])
                tail = bankS[0:TAIL, P:P + TOK]
                dve.tensor_tensor_reduce(out=tail, in0=tail, in1=rowmask[0:TAIL, P:P + TOK], scale=1.0,
                                         scalar=2 * NEG, op0=ALU.add, op1=ALU.max,
                                         accum_out=mx[0:TAIL, img, 1, h:h + 1]).then_inc(freeS, 1)

            def max_out(p, b, img):
                dve.wait_ge(s_m1, 2 * p + img + 1)
                dve.tensor_tensor(mr[:, :], bankS[0:HEADS, 0:TOK], mp[:, 0, :], ALU.subtract).then_inc(freeS, 1)

            def part2(p, b, n):
                dve.wait_ge(s_p1, N_ST * p + n + 1)
                dve.tensor_tensor(p2[:, n % 2, :], p32[:, n % 2, :], p1[:, n % 2, :], ALU.subtract).then_inc(s_p2, 1)

            def heads_out(p, b, n):
                if n % 4 != 3:
                    return
                g, img = (n % HEADS) // 4, n // HEADS
                dve.wait_ge(s_pv, N_ST * p + n + 1)
                if due(8 * p):
                    dve.wait_ge(s_ot, 8 * p)
                for c in range(2):
                    r, t = ROWS[c], 2 * img + c
                    o = bankO[0:r, 4 * VW * c:4 * VW * (c + 1)].rearrange("p (h w) -> p h w", h=4)
                    dve.tensor_reduce(ot[0:r, t, 4 * g:4 * g + 4, :],
                                      o[:, :, 0:3 * HD].rearrange("p h (j d) -> p h d j", j=3), AX.X, ALU.add)
                    ins = dve.reciprocal(rd[0:r, t, 4 * g:4 * g + 4], o[:, :, 3 * HD])
                ins.then_inc(freeO, 1)

            def residual(p, b, m):
                bank, use = USE_C["wo", m]
                dve.wait_ge(s_hc, 16 * (p + 1))
                if due(2 * p):
                    dve.wait_ge(s_ow, 2 * p)
                dve.wait_ge(fullC[bank], N_C[bank] * p + use + 1)
                dve.tensor_tensor(h1[:, m, :], bankC[bank][:, 0:T2], hC[:, m, :], ALU.add).then_inc(freeC[bank], 1)

            def spikes(p, b, k):
                for j in range(STEPS):
                    for m in range(DC):
                        bank, use = USE_C["ffn2", m]
                        y = bankC[bank][:, 0:T2]
                        if j == 0:
                            if due(16 * p):
                                dve.wait_ge(s_out, 16 * p)
                            dve.wait_ge(fullC[bank], N_C[bank] * p + use + 1)
                            ins = dve.tensor_scalar(cn[:, m, :], y, thresholds[0], None, ALU.is_gt)
                        else:
                            dve.wait_ge(s_cn, 8 * p + 2 * (j - 1) + m + 1)
                            ins = dve.scalar_tensor_tensor(out=cn[:, m, :], in0=y, scalar=thresholds[j],
                                                           in1=cn[:, m, :], op0=ALU.is_gt, op1=ALU.add)
                        ins.then_inc(s_cn if j < STEPS - 1 else freeC[bank], 1)
                for m in range(DC):
                    bank, use = USE_C["ffn2", m]
                    dve.wait_ge(freeC[bank], N_C[bank] * (p + 1))
                    dve.scalar_tensor_tensor(out=cn[:, m, :], in0=cn[:, m, :], scalar=1.0 / STEPS, in1=h1[:, m, :],
                                             op0=ALU.mult, op1=ALU.add).then_inc(s_ow, 1)

            run(dve, {
                "stats1": lambda p, b, k: stats(p, bankA, fullA, N_A, st1, mv1, s_bn1, s_ag1),
                "apply1": lambda p, b, k: apply(p, bankA, freeA, mv1, nw1, nt, s_ln1),
                "silu_qk": silu_qk, "silu_v": silu_v, "split_v": split_v, "gate": gate, "q_hat": q_hat,
                "split_q": split_q, "score": score_max, "max_out": max_out, "p": part2, "o": heads_out,
                "wo_out": residual,
                "stats2": lambda p, b, k: stats(p, bankC, fullC, N_C, st2, mv2, s_bn2, s_ag2),
                "apply2": lambda p, b, k: apply(p, bankC, freeC, mv2, nw2, nt, s_ln2),
                "spikes": spikes})

        @block.gpsimd
        def _(pool):
            pool.wait_ge(s_const, 1)

            def newton(v, t, y, s, done):
                if due(done):
                    pool.wait_ge(s, done)
                    pool.nop(nofuse=True)
                pool.tensor_scalar(y.bitcast(I32), v.bitcast(I32), -0.5, RSQRT_SEED, ALU.mult, ALU.add).then_inc(s, 1)
                for k in range(3):
                    pool.wait_ge(s, done + (4 * k + 1))
                    pool.tensor_tensor(t, y, y, ALU.mult).then_inc(s, 1)
                    pool.wait_ge(s, done + (4 * k + 2))
                    pool.tensor_tensor(t, t, v, ALU.mult).then_inc(s, 1)
                    if due(done + (4 * k + 3)):
                        pool.wait_ge(s, done + (4 * k + 3))
                        pool.nop(nofuse=True)
                    pool.tensor_scalar(t, t, -0.5, 1.5, ALU.mult, ALU.add).then_inc(s, 1)
                    pool.wait_ge(s, done + (4 * k + 4))
                    pool.tensor_tensor(y, y, t, ALU.mult).then_inc(s, 1)

            def rstd(p, mv, nw, s_ag, s_ln):
                pool.wait_ge(s_ag, 4 * (p + 1))
                pool.nop(nofuse=True)
                pool.tensor_scalar(nw[:, 0, :], mv[:, :, 1], LN_EPS, None, ALU.add).then_inc(s_ln, 1)
                newton(nw[:, 0, :], nw[:, 2, :], nw[:, 1, :], s_ln, 14 * p + 1)

            def norm_out(p, b, k):
                bank, use = USE_A["norm", 0]
                pool.wait_ge(freeA[bank], N_A[bank] * p + use + 1)
                newton(r2[:, :], nwr[:, 0, :], nwr[:, 1, :], s_rn, 16 * p)
                pool.wait_ge(s_rn, 16 * p + 13)
                pool.nop(nofuse=True)
                pool.tensor_scalar(nwr[:, 0, :], nwr[:, 1, :], NORM_EPS, 0.0, ALU.mult, ALU.add).then_inc(s_rn, 1)
                pool.wait_ge(s_rn, 16 * p + 14)
                pool.nop(nofuse=True)
                pool.tensor_scalar(nwr[:, 1, :], nwr[:, 1, :], NORM_EPS, 1.0, ALU.mult, ALU.add).then_inc(s_rn, 1)

            def gate(p, b, k):
                pool.wait_ge(s_rec, p + 1)
                pool.tensor_tensor(g_sb[:, :], nwr[:, 0, :], r2[:, :], ALU.mult).then_inc(s_rn, 1)

            def split_v(p, b, t):
                r = ROWS[t % 2]
                pool.wait_ge(s_v2, 4 * p + t + 1)
                pool.tensor_tensor(vst[b][0:r, t, :, 2 * HD:3 * HD],
                                   tv[0:r, t, :].rearrange("p (h d) -> p h d", h=HEADS),
                                   vst[b][0:r, t, :, HD:2 * HD], ALU.subtract).then_inc(s_v3, 1)

            def split_q(p, b, c):
                pool.wait_ge(s_q2, 4 * p + c + 1)
                pool.tensor_tensor(parts[2][:, c, :], th[:, c, :], parts[1][:, c, :], ALU.subtract).then_inc(s_q3, 1)

            def max_out(p, b, img):
                pool.wait_ge(s_m2, 2 * p + img + 1)
                pool.tensor_tensor(mp[:, 2, :], mr[:, :], mp[:, 1, :], ALU.subtract).then_inc(s_m3, 1)

            def heads_out(p, b, n):
                if n % 4 != 3:
                    return
                g, img = (n % HEADS) // 4, n // HEADS
                pool.wait_ge(freeO, 8 * p + n // 4 + 1)
                for c in range(2):
                    r, t = ROWS[c], 2 * img + c
                    ins = pool.tensor_tensor(ot[0:r, t, 4 * g:4 * g + 4, :], ot[0:r, t, 4 * g:4 * g + 4, :],
                                             rd[0:r, t, 4 * g:4 * g + 4].unsqueeze(2).broadcast_to([r, 4, HD]),
                                             ALU.mult)
                ins.then_inc(s_ot, 1)

            def square_relu(p, b, f):
                bank, use = USE_C["ffn1", f]
                pool.wait_ge(freeC[bank], N_C[bank] * p + use + 1)
                pool.tensor_tensor(hs[:, f, :], rr[:, f % 2, :], rr[:, f % 2, :], ALU.mult).then_inc(s_hs, 1)

            run(pool, {
                "rstd1": lambda p, b, k: rstd(p, mv1, nw1, s_ag1, s_ln1),
                "norm_out": norm_out, "gate": gate, "split_v": split_v, "split_q": split_q, "max_out": max_out,
                "o": heads_out, "rstd2": lambda p, b, k: rstd(p, mv2, nw2, s_ag2, s_ln2),
                "ffn1_out": square_relu})


def kernel(x, cls_tok, L0_tok_W, L0_tok_b, L0_attn_Wq, L0_attn_Wk, L0_attn_Wv, L0_attn_Wo, L0_attn_q_scale,
           L0_attn_k_scale, L0_ffn_W_fc, L0_ffn_W_proj):
    import concourse.bacc as bacc
    from concourse.bass_utils import run_bass_kernel_spmd

    f = np.float32

    def features(w):
        w = np.asarray(w)
        return np.ascontiguousarray(w.T.reshape(w.shape[1] // P, P, w.shape[0]).transpose(1, 0, 2))

    n = np.asarray(x)
    patches = n.reshape(IMAGES, 3, 14, 16, 14, 16).transpose(0, 1, 2, 4, 3, 5).reshape(PAIRS, 2 * PATCHES, KC, P)
    x_t = np.ascontiguousarray(patches.transpose(0, 3, 2, 1)).reshape(PAIRS, P, KC * 2 * PATCHES)

    i, j = np.arange(P)[:, None], np.arange(P)[None, :]
    row_mask = np.zeros((P, P + TOK), f)
    row_mask[:, :P][j > i] = NEG
    row_mask[:, P:][np.arange(TOK)[None, :] > i + P] = NEG
    key_mask = np.zeros((P, P), f)
    key_mask[i > j] = NEG
    feature = np.arange(P)
    head_rows = np.zeros((P, 4, P), f)
    head_cols = np.zeros((2 * HEADS, 4, P), f)
    for c in range(4):
        head_rows[feature, c, 8 * c + feature % 8] = 1
        head_cols[8 * c + feature % 8, c, feature] = 1

    def per_feature(s):
        return np.ascontiguousarray(np.tile(np.asarray(s).reshape(DC, 8), (1, HD)).T)

    def feature_first(w):
        return np.asarray(w).reshape(DC, 8, HD, D).transpose(0, 2, 1, 3).reshape(D, D)

    arrays = {
        "x_t": x_t,
        "w_tok": features(L0_tok_W),
        "b_tok": np.ascontiguousarray(np.asarray(L0_tok_b).reshape(DC, P).T),
        "cls": np.ascontiguousarray(np.asarray(cls_tok).reshape(DC, P).T),
        "w_qk": features(np.concatenate([feature_first(L0_attn_Wq), feature_first(L0_attn_Wk)], 0)),
        "w_v": features(L0_attn_Wv),
        "w_o": features(L0_attn_Wo),
        "w_fc": features(L0_ffn_W_fc),
        "w_proj": features(L0_ffn_W_proj),
        "q_scale": per_feature(L0_attn_q_scale),
        "k_scale": per_feature(L0_attn_k_scale),
        "eye": np.eye(P, dtype=f),
        "row_mask": row_mask,
        "key_mask": key_mask,
        "head_rows": head_rows,
        "head_cols": head_cols,
    }
    nc = bacc.Bacc("TRN2", target_bir_lowering=False, num_devices=1)
    args = [nc.dram_tensor(name, a.shape, mybir.dt.from_np(a.dtype), kind="ExternalInput").ap()
            for name, a in arrays.items()]
    out_t = nc.dram_tensor("out_t", (PAIRS, P, DC * T2), F32, kind="ExternalOutput").ap()
    program(nc, *args, out_t)
    r = run_bass_kernel_spmd(nc, [arrays], core_ids=[0])
    got = r.results[0]["out_t"].reshape(PAIRS, P, DC, 2, TOK)
    return np.ascontiguousarray(got.transpose(0, 3, 4, 2, 1)).reshape(IMAGES, TOK, D)
```

```python
from contextlib import ExitStack

import numpy as np

import concourse.bass as bass
from concourse import mybir

F32 = mybir.dt.float32
F32R = mybir.dt.float32r
BF16 = mybir.dt.bfloat16
F16 = mybir.dt.float16
I32 = mybir.dt.int32
ALU = mybir.AluOpType
ACT = mybir.ActivationFunctionType
AX = mybir.AxisListType

IMAGES = 64
PAIRS = IMAGES // 2
PATCHES = 196
TOK = PATCHES + 1
T2 = 2 * TOK
D = 256
KIN = 768
HEADS = 16
HD = D // HEADS
FF = 4 * D
P = 128
KC, DC, FC = KIN // P, D // P, FF // P
TAIL = TOK - P
ROWS = (P, TAIL)
VW = 50
NEG = -1e30
LN_EPS = 1e-5
NORM_EPS = 1e-6
RSQRT_SEED = float(0x5F3759DF)
Q_PARTS = (0, 0, 1, 1, 0, 2)
K_PARTS = (0, 1, 0, 1, 2, 0)
KROWS = HD * len(Q_PARTS)
STEPS, BETA, THRESHOLD = 5, 0.9, 1.0

USE_A = {("embed", 0): (0, 0), ("embed", 1): (1, 0), ("turn", 0): (0, 1), ("turn", 1): (1, 1),
         ("back", 0): (0, 2), ("back", 1): (1, 2), ("qk", 0): (0, 3), ("qk", 1): (1, 3),
         ("qk", 2): (0, 4), ("qk", 3): (1, 4), ("norm", 0): (0, 5), ("g", 0): (1, 5), ("g", 1): (0, 6),
         ("g", 2): (1, 6), ("g", 3): (0, 7), ("v", 0): (1, 7), ("v", 1): (0, 8), ("v", 2): (1, 8), ("v", 3): (0, 9)}
N_A = (10, 9)
USE_C = {("wo", 0): (0, 0), ("wo", 1): (1, 0), ("turn", 0): (0, 1), ("turn", 1): (1, 1),
         ("back", 0): (0, 2), ("back", 1): (1, 2), ("ffn2", 0): (0, 7), ("ffn2", 1): (1, 7)}
USE_C.update({("ffn1", f): (f % 2, 3 + f // 2) for f in range(FC)})
N_C = (8, 8)
N_S = 2 * (HEADS + 1)
N_ST = 2 * HEADS
USE_O = {g: (g % 2, g // 2 + (g > 3) * (g % 2)) for g in range(8)}
USE_OT = (2, 5)
N_O = (4, 6)


def place(h):
    return 2 * (h % 8) + h // 8


def spike_thresholds():
    f = np.float32

    def count(y):
        mem, n = f(0), 0
        for _ in range(STEPS):
            mem = f(f(f(BETA) * mem) + y) - f(mem - f(THRESHOLD) > 0)
            n += int(mem - f(THRESHOLD) > 0)
        return n

    out = []
    for want in range(1, STEPS + 1):
        lo, hi = int(f(0.01).view(np.int32)), int(f(2.0).view(np.int32))
        while hi - lo > 1:
            mid = (lo + hi) // 2
            if count(np.int32(mid).view(np.float32)) >= want:
                hi = mid
            else:
                lo = mid
        out.append(float(np.int32(lo).view(np.float32)))
    return out


SHIFT = 2
BEHIND = HEADS + 4


def head_at(slot, behind):
    n, lag = slot - SHIFT - behind, 0
    if n < 0:
        n, lag = n + 2 * HEADS, -1
    return n, lag


def order():
    first = {s: [] for s in range(2 * HEADS)}
    last = {s: [] for s in range(2 * HEADS)}

    def put(where, slot, step, k, lag):
        where[slot].append((step, k, lag))

    for k in range(3):
        put(first, 29 + k, "embed_mm", k, 2)
        put(first, k, "embed_mm", 3 + k, 1)
    put(first, 0, "embed_out", 0, 1)
    put(last, 2, "embed_out", 1, 1)
    put(first, 4, "load_x", 0, 2)
    for img in range(2):
        put(first, 4, "turn1_mm", img, 1)
    put(last, 4, "stats1", 0, 1)
    put(last, 4, "rstd1", 0, 1)
    put(last, 7, "apply1", 0, 1)
    for m in range(DC):
        put(first, 8, "back1_mm", m, 1)
        put(last, 8, "back1_out", m, 1)
    for c in range(4):
        put(first, 10 + c, "qk_mm", c, 1)
        put(last, 10 + c, "silu_qk", c, 1)
        put(last, 11 + c, "square", c, 1)
    put(first, 15, "norm_mm", 0, 1)
    put(last, 15, "norm_out", 0, 1)
    put(last, 19, "gate", 0, 1)
    for c in range(4):
        put(first, 20 + c // 2, "g_mm", c, 1)
        put(last, 20 + c // 2, "q_hat", c, 1)
        put(last, 21 + c // 2, "split_q", c, 1)
    put(last, 23, "restack", 0, 1)
    for t in range(4):
        put(first, 23 + t, "v_mm", t, 1)
        put(last, 23 + t, "silu_v", t, 1)
        put(last, 25 + t, "split_v", t, 1)

    put(first, 10, "ot_mm", 0, -1)
    put(last, 10, "ot_out", 0, -1)
    put(first, 26, "ot_mm", 1, -1)
    put(first, 26, "ot_out", 1, -1)
    for m in range(DC):
        put(first, 27 + m, "wo_mm", m, -1)
        put(last, 27 + m, "wo_out", m, -1)
    put(last, 28, "keep_h", 0, 0)
    for img in range(2):
        put(first, 30, "turn2_mm", img, -1)
    put(last, 30, "stats2", 0, -1)
    put(last, 30, "rstd2", 0, -1)
    put(first, 1, "apply2", 0, -2)
    for m in range(DC):
        put(first, 2, "back2_mm", m, -2)
        put(first, 2, "back2_out", m, -2)
    for f in range(FC):
        slot = (3, 5, 6, 7, 8, 9, 13, 14)[f]
        put(first, slot, "ffn1_mm", f, -2)
        put(last, slot, "ffn1_out", f, -2)
    for k in range(8):
        put(first, 15 + k, "ffn2_mm", k, -2)
    for m in range(DC):
        for j in range(STEPS + 1):
            put(last, 18 + 4 * m + j // 2, "spikes", (STEPS + 1) * m + j, -2)
    put(last, 26, "store", 0, -2)

    out = []
    for s in range(2 * HEADS):
        out += first[s]
        if s % HEADS == SHIFT:
            for step in ("max_mm", "max_out"):
                out.append((step, 1, -1) if s < HEADS else (step, 0, 0))
        for step, behind in (("score", 0), ("st", BEHIND), ("p", BEHIND + 1), ("pv", BEHIND + 2), ("o", BEHIND + 3)):
            out.append((step, *head_at(s, behind)))
        out += last[s]
    return out


ORDER = order()
LOOP_FROM = 4


def program(nc, x_t, w_tok, b_tok, cls, w_qk, w_v, w_o, w_fc, w_proj, q_scale, k_scale,
            eye, row_mask, key_mask, head_rows, head_cols, out_t):
    thresholds = spike_thresholds()
    with ExitStack() as ctx:
        def sb(name, shape, dt=F32):
            return ctx.enter_context(nc.sbuf_tensor(name, shape, dt))

        def psum(name):
            return ctx.enter_context(nc.psum_tensor(name, [P, 512], F32))

        def sem(name):
            return ctx.enter_context(nc.semaphore(name))

        wtok = sb("wtok", [P, KC, D])
        btok = sb("btok", [P, DC])
        clsT = sb("clsT", [P, DC])
        wqk = sb("wqk", [P, DC, 2 * D])
        wv = sb("wv", [P, DC, D])
        wo = sb("wo", [P, DC, D])
        wfc = sb("wfc", [P, DC, FF])
        wproj = sb("wproj", [P, FC, D])
        qsc = sb("qsc", [P, DC])
        ksc = sb("ksc", [P, DC])
        sc = sb("sc", [P, 4])
        eyef = sb("eyef", [P, P])
        eyeb = sb("eyeb", [P, P], BF16)
        rowmask = sb("rowmask", [P, P + TOK])
        keymask = sb("keymask", [P, P], BF16)
        hrows = sb("hrows", [P, 4, P], F32R)
        hcols = sb("hcols", [2 * HEADS, 4, P], F32R)

        x_sb = sb("x_sb", [P, KC, 2 * PATCHES])
        hA = [sb(f"hA{b}", [P, DC, 2, TOK]) for b in range(2)]
        hC = sb("hC", [P, DC, T2])
        st1 = sb("st1", [P, 4, 6])
        mv1 = sb("mv1", [P, 4, 2])
        nw1 = sb("nw1", [P, 3, 4])
        nt = sb("nt", [P, 4, D])
        lnT = sb("lnT", [P, DC, T2])
        th = sb("th", [P, 4, T2])
        s2 = sb("s2", [P, 4, T2])
        sq = sb("sq", [P, 4, T2], F32R)
        r2 = sb("r2", [2 * HEADS, T2])
        nwr = sb("nwr", [2 * HEADS, 2, T2])
        g_sb = sb("g_sb", [2 * HEADS, T2], F32R)
        parts = [sb(f"part{j}", [P, 4, T2], BF16) for j in range(3)]
        tv = sb("tv", [P, 4, D])
        v2 = sb("v2", [P, 4, D])
        qst = [sb(f"qst{b}", [KROWS + 3, HEADS, T2], BF16) for b in range(2)]
        kst = [sb(f"kst{b}", [KROWS + 3, HEADS * T2 + 64], BF16) for b in range(2)]
        vst = [sb(f"vst{b}", [P, 4, HEADS, VW], BF16) for b in range(2)]
        mx = sb("mx", [P, 2, 2, HEADS])
        mr = sb("mr", [HEADS, TOK])
        mp = sb("mp", [HEADS, 3, TOK], BF16)
        p32 = sb("p32", [P, 2, TOK + TAIL])
        p1 = sb("p1", [P, 2, TOK + TAIL], F16)
        p2 = sb("p2", [P, 2, TOK + TAIL], F16)
        rd = sb("rd", [P, 4, HEADS])
        ot = sb("ot", [P, 4, HEADS, HD])
        oT = sb("oT", [P, DC, 2, TOK])
        h1 = sb("h1", [P, DC, T2])
        st2 = sb("st2", [P, 4, 6])
        mv2 = sb("mv2", [P, 4, 2])
        nw2 = sb("nw2", [P, 3, 4])
        l2T = sb("l2T", [P, DC, T2])
        rr = sb("rr", [P, 2, T2])
        hs = sb("hs", [P, FC, T2])
        cn = sb("cn", [P, DC, T2])
        hrowsf = hs[:, 0:4, 0:P]
        hcolsf = hs[0:2 * HEADS, 4:8, 0:P]
        keymaskf = hs[:, 0, P:2 * P]

        bankA = [psum("bankA0"), psum("bankA1")]
        bankC = [psum("bankC0"), psum("bankC1")]
        bankS, bankST, bankO = psum("bankS"), psum("bankST"), [psum("bankO0"), psum("bankO1")]

        fullA, freeA = [sem("fullA0"), sem("fullA1")], [sem("freeA0"), sem("freeA1")]
        fullC, freeC = [sem("fullC0"), sem("fullC1")], [sem("freeC0"), sem("freeC1")]
        fullS, freeS = sem("fullS"), sem("freeS")
        fullST, freeST = sem("fullST"), sem("freeST")
        freeO = [sem("freeO0"), sem("freeO1")]
        full_ot = sem("heads_turned")
        s_w = sem("weights_in")
        s_const = sem("constants_ready")
        s_x = sem("x_in")
        s_hc = sem("h_kept")
        s_bn1, s_ag1, s_ln1 = sem("bn_stats_1"), sem("bn_aggr_1"), sem("rstd_1_steps")
        s_bn2, s_ag2, s_ln2 = sem("bn_stats_2"), sem("bn_aggr_2"), sem("rstd_2_steps")
        s_th, s_sq = sem("tanh_qk"), sem("squares")
        s_rn, s_rec = sem("norm_steps"), sem("norm_reciprocal")
        s_q1, s_r1, s_q2, s_q3 = sem("qk_part1"), sem("qk_rest"), sem("qk_part2"), sem("qk_part3")
        s_tv, s_v1, s_rv, s_v2, s_v3 = sem("tanh_v"), sem("v_part1"), sem("v_rest"), sem("v_part2"), sem("v_part3")
        s_stack = sem("stack_in")
        s_m1, s_m2, s_m3, s_mrow = sem("max_part1"), sem("max_part2"), sem("max_part3"), sem("max_rows_in")
        s_p1, s_p2, s_pv = sem("p_part1"), sem("p_part2"), sem("pv_done")
        s_ot = sem("heads_divided")
        s_hs = sem("ffn_hidden")
        s_cn, s_ow, s_out = sem("count_steps"), sem("out_ready"), sem("out_stored")

        block = ctx.enter_context(nc.Block())

        def due(count):
            return not isinstance(count, int) or count > 0

        def run(eng, mine):
            def peeled(i):
                for step, k, lag in ORDER:
                    if step in mine and 0 <= i + lag < PAIRS:
                        mine[step](i + lag, (i + lag) % 2, k)

            for i in range(-2, LOOP_FROM):
                peeled(i)
            with eng.Fori(LOOP_FROM, PAIRS - 3, 2) as i:
                for u in range(2):
                    for step, k, lag in ORDER:
                        if step in mine:
                            mine[step](i + (u + lag), (LOOP_FROM + u + lag) % 2, k)
            for i in range(PAIRS - 2, PAIRS + 2):
                peeled(i)

        @block.sync
        def _(sp):
            loads = [(wtok[:, :, :], w_tok), (btok[:, :], b_tok), (clsT[:, :], cls), (eyef[:, :], eye),
                     (wqk[:, :, :], w_qk), (wv[:, :, :], w_v), (hrowsf, head_rows), (hcolsf, head_cols),
                     (qsc[:, :], q_scale), (ksc[:, :], k_scale), (rowmask[:, :], row_mask),
                     (keymaskf, key_mask), (wo[:, :, :], w_o), (wfc[:, :, :], w_fc), (wproj[:, :, :], w_proj)]
            for dst, src in loads:
                sp.dma_start(dst, src).then_inc(s_w, 16)

            def load_x(p, b, k):
                if due(N_A[1] * (p - 1) + 1):
                    sp.wait_ge(fullA[1], N_A[1] * (p - 1) + 1)
                sp.dma_start(x_sb[:, :, :], x_t[p].rearrange("p (k n) -> p k n", k=KC)).then_inc(s_x, 16)

            def keep_h(p, b, k):
                sp.wait_ge(freeA[0], N_A[0] * p + 1)
                sp.wait_ge(freeA[1], N_A[1] * p + 1)
                if due(N_C[0] * (p - 1) + 1):
                    sp.wait_ge(freeC[0], N_C[0] * (p - 1) + 1)
                if due(N_C[1] * (p - 1) + 1):
                    sp.wait_ge(freeC[1], N_C[1] * (p - 1) + 1)
                sp.dma_start(hC[:, :, :], hA[b][:, :, :, :].rearrange("p c i n -> p c (i n)")).then_inc(s_hc, 16)

            def restack(p, b, k):
                if due(N_ST * (p - 1)):
                    sp.wait_ge(fullST, N_ST * (p - 1))
                    sp.nop(nofuse=True)
                sp.wait_ge(s_q1, 4 * (p + 1))
                sp.wait_ge(s_q2, 4 * (p + 1))
                sp.wait_ge(s_q3, 4 * (p + 1))
                for j in range(len(Q_PARTS)):
                    rows = slice(HD * j, HD * (j + 1))
                    sp.dma_start(qst[b][rows, :, :], parts[Q_PARTS[j]][:, 0:2, :]).then_inc(s_stack, 16)
                    sp.dma_start(kst[b][rows, 0:HEADS * T2], parts[K_PARTS[j]][:, 2:4, :]).then_inc(s_stack, 16)

            def max_rows(p, b, img):
                sp.wait_ge(s_m3, 2 * p + img + 1)
                for j in range(3):
                    sp.dma_start(qst[b][KROWS + j:KROWS + j + 1, :, img * TOK:(img + 1) * TOK],
                                 mp[:, j, :]).then_inc(s_mrow, 16)

            def store(p, b, k):
                sp.wait_ge(s_ow, 2 * (p + 1))
                sp.dma_start(out_t[p].rearrange("p (c n) -> p c n", c=DC), cn[:, :, :]).then_inc(s_out, 16)

            run(sp, {"load_x": load_x, "keep_h": keep_h, "restack": restack, "max_out": max_rows, "store": store})
            sp.wait_ge(s_out, 16 * PAIRS)

        @block.tensor
        def _(pe):
            pe.wait_ge(s_const, 1)
            pe.wait_ge(s_w, 16 * 15)

            def embed(p, b, third):
                m, third = divmod(third, 3)
                bank, use = USE_A["embed", m]
                if third == 0:
                    pe.wait_ge(s_x, 16 * (p + 1))
                    if due(N_A[bank] * p + use):
                        pe.wait_ge(freeA[bank], N_A[bank] * p + use)
                for k in range(2 * third, 2 * third + 2):
                    mm = pe.matmul(bankA[bank][:, 0:2 * PATCHES], wtok[:, k, m * P:(m + 1) * P], x_sb[:, k, :],
                                   start=(k == 0), stop=(k == KC - 1))
                if third == 2:
                    mm.then_inc(fullA[bank], 1)

            def turn(p, img, src, banks, full, free, per, uses):
                bank, use = uses["turn", img]
                pe.wait_ge(free[0], per[0] * p + 1)
                pe.wait_ge(free[1], per[1] * p + 1)
                for c in range(2):
                    for m in range(DC):
                        n0 = c * P
                        mm = pe.transpose(banks[bank][0:ROWS[c], c * D + m * P:c * D + (m + 1) * P],
                                          src(m, img, n0, n0 + ROWS[c]), eyef[:, :])
                mm.then_inc(full[bank], 1)

            def back(p, m, src, banks, full, free, per, uses):
                bank, use = uses["back", m]
                pe.wait_ge(free[0], per[0] * p + 2)
                pe.wait_ge(free[1], per[1] * p + 2)
                for t in range(4):
                    n0 = (t // 2) * TOK + (t % 2) * P
                    r = ROWS[t % 2]
                    mm = pe.transpose(banks[bank][:, n0:n0 + r], src[0:r, t, m * P:(m + 1) * P], eyef[0:r, 0:r])
                mm.then_inc(full[bank], 1)

            def qk(p, b, c):
                bank, use = USE_A["qk", c]
                pe.wait_ge(freeA[1 - bank], N_A[1 - bank] * p + 3)
                if due(N_A[bank] * p + use):
                    pe.wait_ge(freeA[bank], N_A[bank] * p + use)
                for k in range(DC):
                    mm = pe.matmul(bankA[bank][:, 0:T2], wqk[:, k, c * P:(c + 1) * P], lnT[:, k, :],
                                   start=(k == 0), stop=(k == DC - 1))
                mm.then_inc(fullA[bank], 1)

            def v(p, b, t):
                bank, use = USE_A["v", t]
                n0, r = (t // 2) * TOK + (t % 2) * P, ROWS[t % 2]
                if due(N_A[bank] * p + use):
                    pe.wait_ge(freeA[bank], N_A[bank] * p + use)
                for k in range(DC):
                    mm = pe.matmul(bankA[bank][0:r, 0:D], lnT[:, k, n0:n0 + r], wv[:, k, :],
                                   start=(k == 0), stop=(k == DC - 1))
                mm.then_inc(fullA[bank], 1)

            def norm(p, b, _k):
                bank, use = USE_A["norm", 0]
                pe.wait_ge(s_sq, 4 * (p + 1))
                if due(N_A[bank] * p + use):
                    pe.wait_ge(freeA[bank], N_A[bank] * p + use)
                for c in range(4):
                    mm = pe.matmul(bankA[bank][:, 0:T2], hrows[:, c, :], sq[:, c, :], start=(c == 0), stop=(c == 3))
                mm.then_inc(fullA[bank], 1)

            def g(p, b, c):
                bank, use = USE_A["g", c]
                pe.wait_ge(s_rn, 12 * (p + 1))
                if due(N_A[bank] * p + use):
                    pe.wait_ge(freeA[bank], N_A[bank] * p + use)
                pe.matmul(bankA[bank][:, 0:T2], hcols[:, c, :], g_sb[:, :], start=True,
                          stop=True).then_inc(fullA[bank], 1)

            def score(p, b, s):
                img, h = s // HEADS, s % HEADS
                if s == 0:
                    pe.wait_ge(s_stack, 16 * 12 * (p + 1))
                if due(N_S * p + img * (HEADS + 1) + h):
                    pe.wait_ge(freeS, N_S * p + img * (HEADS + 1) + h)
                at = place(h)
                q0, k0 = img * TOK, at * T2 + img * TOK
                pe.matmul(bankS[:, 0:P], qst[b][0:KROWS, at, q0:q0 + P], kst[b][0:KROWS, k0:k0 + P],
                          start=True, stop=True)
                pe.matmul(bankS[0:TAIL, P:P + TOK], qst[b][0:KROWS, at, q0 + P:q0 + TOK],
                          kst[b][0:KROWS, k0:k0 + TOK], start=True, stop=True).then_inc(fullS, 1)

            def max_turn(p, b, img):
                use = N_S * p + img * (HEADS + 1) + HEADS
                if due(use):
                    pe.wait_ge(freeS, use)
                pe.transpose(bankS[0:HEADS, 0:P], mx[:, img, 0, :], eyef[:, :])
                pe.transpose(bankS[0:HEADS, P:TOK], mx[0:TAIL, img, 1, :], eyef[0:TAIL, 0:TAIL]).then_inc(fullS, 1)

            def st(p, b, n):
                img, h = n // HEADS, n % HEADS
                if h == 0:
                    if due(16 * 3 * (2 * p + img + 1)):
                        pe.wait_ge(s_mrow, 16 * 3 * (2 * p + img + 1))
                if due(N_ST * p + n):
                    pe.wait_ge(freeST, N_ST * p + n)
                at = place(h)
                q0, k0 = img * TOK, at * T2 + img * TOK
                pe.matmul(bankST[:, 0:TOK], kst[b][:, k0:k0 + P], qst[b][:, at, q0:q0 + TOK], start=True, stop=False,
                          skip_group_check=True)
                pe.matmul(bankST[:, 0:P], eyeb[:, :], keymask[:, :], start=False, stop=True, skip_group_check=True)
                pe.matmul(bankST[:, TOK:TOK + TAIL], kst[b][:, k0 + P:k0 + 2 * P], qst[b][:, at, q0 + P:q0 + TOK],
                          start=True, stop=False, skip_group_check=True)
                pe.matmul(bankST[:, TOK:TOK + TAIL], eyeb[:, :], keymask[:, 0:TAIL], start=False, stop=True,
                          skip_group_check=True).then_inc(fullST, 1)

            def pv(p, b, n):
                img, h = n // HEADS, n % HEADS
                if n == 0:
                    pe.wait_ge(s_v2, 4 * (p + 1))
                    pe.wait_ge(s_v3, 4 * (p + 1))
                pe.wait_ge(s_p2, N_ST * p + n + 1)
                bank, use = USE_O[n // 4]
                if n % 4 == 0 and due(N_O[bank] * p + use):
                    pe.wait_ge(freeO[bank], N_O[bank] * p + use)
                w, hh, t = n % 2, h % 4, 2 * img
                o0 = bankO[bank][:, hh * VW:(hh + 1) * VW]
                o1 = bankO[bank][0:TAIL, (4 + hh) * VW:(5 + hh) * VW]
                pe.matmul(o0, p1[:, w, 0:P], vst[b][:, t, h, :], start=True, stop=False, skip_group_check=True)
                pe.matmul(o0, p2[:, w, 0:P], vst[b][:, t, h, :], start=False, stop=True, skip_group_check=True)
                pe.matmul(o1, p1[:, w, P:TOK], vst[b][:, t, h, :], start=True, stop=False, skip_group_check=True)
                pe.matmul(o1, p2[:, w, P:TOK], vst[b][:, t, h, :], start=False, stop=False, skip_group_check=True)
                pe.matmul(o1, p1[0:TAIL, w, TOK:], vst[b][0:TAIL, t + 1, h, :], start=False, stop=False,
                          skip_group_check=True)
                pe.matmul(o1, p2[0:TAIL, w, TOK:], vst[b][0:TAIL, t + 1, h, :], start=False, stop=True,
                          skip_group_check=True).then_inc(s_pv, 1)

            def ot_turn(p, b, img):
                pe.wait_ge(s_ot, 8 * p + 4 * (img + 1))
                pe.wait_ge(freeO[1], N_O[1] * p + USE_OT[img])
                for m in range(DC):
                    for c in range(2):
                        r = ROWS[c]
                        mm = pe.transpose(bankO[1][:, m * TOK + c * P:m * TOK + c * P + r],
                                          ot[0:r, 2 * img + c, 8 * m:8 * (m + 1), :].rearrange("p h d -> p (h d)"),
                                          eyef[0:r, 0:r])
                mm.then_inc(full_ot, 1)

            def project(p, b, m):
                bank, use = USE_C["wo", m]
                pe.wait_ge(freeO[1], N_O[1] * (p + 1))
                if due(N_C[bank] * p + use):
                    pe.wait_ge(freeC[bank], N_C[bank] * p + use)
                for k in range(DC):
                    mm = pe.matmul(bankC[bank][:, 0:T2], wo[:, k, m * P:(m + 1) * P],
                                   oT[:, k, :, :].rearrange("p i n -> p (i n)"), start=(k == 0), stop=(k == DC - 1))
                mm.then_inc(fullC[bank], 1)

            def ffn1(p, b, f):
                bank, use = USE_C["ffn1", f]
                pe.wait_ge(freeC[1 - bank], N_C[1 - bank] * p + 3)
                if due(N_C[bank] * p + use):
                    pe.wait_ge(freeC[bank], N_C[bank] * p + use)
                for k in range(DC):
                    mm = pe.matmul(bankC[bank][:, 0:T2], wfc[:, k, f * P:(f + 1) * P], l2T[:, k, :],
                                   start=(k == 0), stop=(k == DC - 1))
                mm.then_inc(fullC[bank], 1)

            def ffn2(p, b, quarter):
                m, quarter = divmod(quarter, 4)
                bank, use = USE_C["ffn2", m]
                if quarter == 0:
                    pe.wait_ge(s_hs, FC * (p + 1))
                    pe.wait_ge(freeC[bank], N_C[bank] * p + use)
                for f in range(2 * quarter, 2 * quarter + 2):
                    mm = pe.matmul(bankC[bank][:, 0:T2], wproj[:, f, m * P:(m + 1) * P], hs[:, f, :],
                                   start=(f == 0), stop=(f == FC - 1))
                if quarter == 3:
                    mm.then_inc(fullC[bank], 1)

            run(pe, {
                "embed_mm": embed,
                "turn1_mm": lambda p, b, k: turn(p, k, lambda m, i, a, e: hA[b][:, m, i, a:e],
                                                 bankA, fullA, freeA, N_A, USE_A),
                "back1_mm": lambda p, b, k: back(p, k, nt, bankA, fullA, freeA, N_A, USE_A),
                "qk_mm": qk, "v_mm": v, "norm_mm": norm, "g_mm": g,
                "score": score, "max_mm": max_turn, "st": st, "pv": pv, "ot_mm": ot_turn, "wo_mm": project,
                "turn2_mm": lambda p, b, k: turn(p, k, lambda m, i, a, e: h1[:, m, i * TOK + a:i * TOK + e],
                                                 bankC, fullC, freeC, N_C, USE_C),
                "back2_mm": lambda p, b, k: back(p, k, nt, bankC, fullC, freeC, N_C, USE_C),
                "ffn1_mm": ffn1, "ffn2_mm": ffn2})

        @block.scalar
        def _(act):
            act.wait_ge(s_w, 16 * 15)
            act.wait_ge(s_const, 1)

            def embed_out(p, b, m):
                bank, use = USE_A["embed", m]
                if due(16 * (p - 1)):
                    act.wait_ge(s_hc, 16 * (p - 1))
                act.wait_ge(fullA[bank], N_A[bank] * p + use + 1)
                act.activation(hA[b][:, m, :, 1:TOK], bankA[bank][:, 0:2 * PATCHES].rearrange("p (i n) -> p i n", i=2),
                               ACT.Identity, bias=btok[:, m:m + 1]).then_inc(freeA[bank], 1)

            def back_out(p, m, dst, banks, full, free, per, uses):
                bank, use = uses["back", m]
                act.wait_ge(full[bank], per[bank] * p + use + 1)
                act.activation(dst[:, m, :], banks[bank][:, 0:T2], ACT.Copy).then_inc(free[bank], 1)

            def tanh_qk(p, b, c):
                bank, use = USE_A["qk", c]
                if due(4 * p):
                    act.wait_ge(s_q3, 4 * p)
                act.wait_ge(fullA[bank], N_A[bank] * p + use + 1)
                act.activation(th[:, c, :], bankA[bank][:, 0:T2], ACT.Tanh, scale=0.5).then_inc(s_th, 1)

            def square(p, b, c):
                bank, use = USE_A["qk", c]
                act.wait_ge(freeA[bank], N_A[bank] * p + use + 1)
                act.activation(sq[:, c, :], s2[:, c, :], ACT.Square, scale=0.5).then_inc(s_sq, 1)

            def norm_out(p, b, k):
                bank, use = USE_A["norm", 0]
                if due(12 * p):
                    act.wait_ge(s_rn, 12 * p)
                act.wait_ge(fullA[bank], N_A[bank] * p + use + 1)
                act.activation(r2[:, :], bankA[bank][0:2 * HEADS, 0:T2], ACT.Copy).then_inc(freeA[bank], 1)

            def tanh_v(p, b, t):
                bank, use = USE_A["v", t]
                r = ROWS[t % 2]
                if due(4 * p):
                    act.wait_ge(s_v3, 4 * p)
                act.wait_ge(fullA[bank], N_A[bank] * p + use + 1)
                act.activation(tv[0:r, t, :], bankA[bank][0:r, 0:D], ACT.Tanh, scale=0.5).then_inc(s_tv, 1)

            def split_v(p, b, t):
                bank, use = USE_A["v", t]
                r = ROWS[t % 2]
                heads = lambda a: a[0:r, t, :].rearrange("p (h d) -> p h d", h=HEADS)
                if due(N_ST * (p - 1)):
                    act.wait_ge(s_pv, N_ST * (p - 1))
                act.wait_ge(freeA[bank], N_A[bank] * p + use + 1)
                act.activation(vst[b][0:r, t, :, 0:HD], heads(v2), ACT.Copy).then_inc(s_v1, 1)
                act.wait_ge(s_rv, 4 * p + t + 1)
                act.activation(vst[b][0:r, t, :, HD:2 * HD], heads(tv), ACT.Copy).then_inc(s_v2, 1)

            def split_q(p, b, c):
                bank, use = USE_A["g", c]
                if due(16 * 12 * p):
                    act.wait_ge(s_stack, 16 * 12 * p)
                act.wait_ge(freeA[bank], N_A[bank] * p + use + 1)
                act.activation(parts[0][:, c, :], th[:, c, :], ACT.Copy, scale=sc[:, c:c + 1]).then_inc(s_q1, 1)
                act.wait_ge(s_r1, 4 * p + c + 1)
                act.activation(parts[1][:, c, :], th[:, c, :], ACT.Copy).then_inc(s_q2, 1)

            def max_out(p, b, img):
                if due(16 * 3 * (2 * p + img)):
                    act.wait_ge(s_mrow, 16 * 3 * (2 * p + img))
                act.wait_ge(fullS, N_S * p + img * (HEADS + 1) + HEADS + 1)
                act.activation(mp[:, 0, :], bankS[0:HEADS, 0:TOK], ACT.Copy).then_inc(s_m1, 1)
                act.wait_ge(freeS, N_S * p + (img + 1) * (HEADS + 1))
                act.activation(mp[:, 1, :], mr[:, :], ACT.Copy).then_inc(s_m2, 1)

            def exp(p, b, n):
                if due(N_ST * p + n - 1):
                    act.wait_ge(s_p2, N_ST * p + n - 1)
                act.wait_ge(fullST, N_ST * p + n + 1)
                act.activation(p32[:, n % 2, :], bankST[:, 0:TOK + TAIL], ACT.Exp).then_inc(freeST, 1)

            def part1(p, b, n):
                if due(N_ST * p + n - 1):
                    act.wait_ge(s_pv, N_ST * p + n - 1)
                act.wait_ge(freeST, N_ST * p + n + 1)
                act.activation(p1[:, n % 2, :], p32[:, n % 2, :], ACT.Copy).then_inc(s_p1, 1)

            def ot_out(p, b, img):
                act.wait_ge(full_ot, 2 * p + img + 1)
                act.activation(oT[:, :, img, :], bankO[1][:, 0:2 * TOK].rearrange("p (m n) -> p m n", m=DC),
                               ACT.Copy).then_inc(freeO[1], 1)

            def relu(p, b, f):
                bank, use = USE_C["ffn1", f]
                if due(FC * p + f - 1):
                    act.wait_ge(s_hs, FC * p + f - 1)
                act.wait_ge(fullC[bank], N_C[bank] * p + use + 1)
                act.activation(rr[:, f % 2, :], bankC[bank][:, 0:T2], ACT.Relu).then_inc(freeC[bank], 1)

            run(act, {
                "embed_out": embed_out,
                "back1_out": lambda p, b, k: back_out(p, k, lnT, bankA, fullA, freeA, N_A, USE_A),
                "silu_qk": tanh_qk, "square": square, "norm_out": norm_out, "silu_v": tanh_v, "split_v": split_v,
                "split_q": split_q, "max_out": max_out, "st": exp, "p": part1, "ot_out": ot_out,
                "back2_out": lambda p, b, k: back_out(p, k, l2T, bankC, fullC, freeC, N_C, USE_C),
                "ffn1_out": relu})

        @block.vector
        def _(dve):
            dve.wait_ge(s_w, 16 * 15)
            for b in range(2):
                dve.memset(kst[b][:, HEADS * T2:], 0.0)
                dve.memset(kst[b][KROWS:KROWS + 3, 0:HEADS * T2], -1.0)
                dve.memset(vst[b][:, :, :, 3 * HD:3 * HD + 1], 2.0)
                dve.memset(vst[b][:, :, :, 3 * HD + 1:], 0.0)
            dve.memset(mv1[:, :, :], 1.0)
            dve.memset(mv2[:, :, :], 1.0)
            dve.tensor_copy(eyeb[:, :], eyef[:, :])
            dve.tensor_copy(keymask[:, :], keymaskf)
            dve.tensor_copy(hrows[:, :, :], hrowsf)
            dve.tensor_copy(hcols[:, :, :], hcolsf)
            for b in range(2):
                for img in range(2):
                    dve.tensor_copy(hA[b][:, :, img, 0], clsT[:, :])
            dve.memset(sc[:, 2:4], 1.0)
            dve.scalar_tensor_tensor(out=sc[:, 0:2], in0=qsc[:, :], scalar=0.25, in1=ksc[:, :],
                                     op0=ALU.mult, op1=ALU.mult).then_inc(s_const, 1)

            def stats(p, banks, full, per, st, mv, s_bn, s_ag):
                for t in range(4):
                    img, r = t // 2, ROWS[t % 2]
                    dve.wait_ge(full[img], per[img] * p + 2)
                    dve.bn_stats(st[0:r, t, :], banks[img][0:r, (t % 2) * D:(t % 2 + 1) * D]).then_inc(s_bn, 1)
                for t in range(4):
                    r = ROWS[t % 2]
                    dve.wait_ge(s_bn, 4 * p + t + 1)
                    dve.nop(nofuse=True)
                    dve.bn_aggr(mv[0:r, t, :], st[0:r, t, :]).then_inc(s_ag, 1)

            def apply(p, banks, free, mv, nw, dst, s_ln):
                dve.wait_ge(s_ln, 14 * (p + 1))
                for t in range(4):
                    img, r = t // 2, ROWS[t % 2]
                    ins = dve.tensor_scalar(dst[0:r, t, :], banks[img][0:r, (t % 2) * D:(t % 2 + 1) * D],
                                            mv[0:r, t, 0:1], nw[0:r, 1, t:t + 1], ALU.subtract, ALU.mult)
                    if t % 2:
                        ins.then_inc(free[img], 1)

            def silu_qk(p, b, c):
                bank, use = USE_A["qk", c]
                dve.wait_ge(s_th, 4 * p + c + 1)
                dve.scalar_tensor_tensor(out=s2[:, c, :], in0=th[:, c, :], scalar=1.0, in1=bankA[bank][:, 0:T2],
                                         op0=ALU.add, op1=ALU.mult).then_inc(freeA[bank], 1)

            def silu_v(p, b, t):
                bank, use = USE_A["v", t]
                r = ROWS[t % 2]
                dve.wait_ge(s_tv, 4 * p + t + 1)
                dve.scalar_tensor_tensor(out=v2[0:r, t, :], in0=tv[0:r, t, :], scalar=1.0, in1=bankA[bank][0:r, 0:D],
                                         op0=ALU.add, op1=ALU.mult).then_inc(freeA[bank], 1)

            def split_v(p, b, t):
                r = ROWS[t % 2]
                dve.wait_ge(s_v1, 4 * p + t + 1)
                dve.tensor_tensor(tv[0:r, t, :].rearrange("p (h d) -> p h d", h=HEADS),
                                  v2[0:r, t, :].rearrange("p (h d) -> p h d", h=HEADS),
                                  vst[b][0:r, t, :, 0:HD], ALU.subtract).then_inc(s_rv, 1)

            def gate(p, b, k):
                dve.wait_ge(s_rn, 12 * p + 11)
                dve.reciprocal(r2[:, :], nwr[:, 1, :]).then_inc(s_rec, 1)

            def q_hat(p, b, c):
                bank, use = USE_A["g", c]
                dve.wait_ge(fullA[bank], N_A[bank] * p + use + 1)
                dve.scalar_tensor_tensor(out=th[:, c, :], in0=bankA[bank][:, 0:T2], scalar=1.0, in1=s2[:, c, :],
                                         op0=ALU.subtract, op1=ALU.mult).then_inc(freeA[bank], 1)

            def split_q(p, b, c):
                dve.wait_ge(s_q1, 4 * p + c + 1)
                dve.scalar_tensor_tensor(out=th[:, c, :], in0=th[:, c, :], scalar=sc[:, c:c + 1],
                                         in1=parts[0][:, c, :], op0=ALU.mult, op1=ALU.subtract).then_inc(s_r1, 1)

            def score_max(p, b, s):
                img, h = s // HEADS, s % HEADS
                at = place(h)
                dve.wait_ge(fullS, N_S * p + img * (HEADS + 1) + h + 1)
                dve.nop(nofuse=True)
                dve.tensor_tensor_reduce(out=bankS[:, 0:P], in0=bankS[:, 0:P], in1=rowmask[:, 0:P], scale=1.0,
                                         scalar=2 * NEG, op0=ALU.add, op1=ALU.max, accum_out=mx[:, img, 0, at:at + 1])
                tail = bankS[0:TAIL, P:P + TOK]
                dve.tensor_tensor_reduce(out=tail, in0=tail, in1=rowmask[0:TAIL, P:P + TOK], scale=1.0,
                                         scalar=2 * NEG, op0=ALU.add, op1=ALU.max,
                                         accum_out=mx[0:TAIL, img, 1, at:at + 1]).then_inc(freeS, 1)

            def max_out(p, b, img):
                dve.wait_ge(s_m1, 2 * p + img + 1)
                dve.tensor_tensor(mr[:, :], bankS[0:HEADS, 0:TOK], mp[:, 0, :], ALU.subtract).then_inc(freeS, 1)

            def part2(p, b, n):
                dve.wait_ge(s_p1, N_ST * p + n + 1)
                dve.tensor_tensor(p2[:, n % 2, :], p32[:, n % 2, :], p1[:, n % 2, :], ALU.subtract).then_inc(s_p2, 1)

            def heads_out(p, b, n):
                if n % 4 != 3:
                    return
                g, img = (n % HEADS) // 4, n // HEADS
                dve.wait_ge(s_pv, N_ST * p + n + 1)
                if due(8 * p):
                    dve.wait_ge(s_ot, 8 * p)
                bank, use = USE_O[n // 4]
                for c in range(2):
                    r, t = ROWS[c], 2 * img + c
                    o = bankO[bank][0:r, 4 * VW * c:4 * VW * (c + 1)].rearrange("p (h w) -> p h w", h=4)
                    dve.tensor_reduce(ot[0:r, t, 4 * g:4 * g + 4, :],
                                      o[:, :, 0:3 * HD].rearrange("p h (j d) -> p h d j", j=3), AX.X, ALU.add)
                    ins = dve.reciprocal(rd[0:r, t, 4 * g:4 * g + 4], o[:, :, 3 * HD])
                ins.then_inc(freeO[bank], 1)

            def residual(p, b, m):
                bank, use = USE_C["wo", m]
                dve.wait_ge(s_hc, 16 * (p + 1))
                if due(2 * p):
                    dve.wait_ge(s_ow, 2 * p)
                dve.wait_ge(fullC[bank], N_C[bank] * p + use + 1)
                dve.tensor_tensor(h1[:, m, :], bankC[bank][:, 0:T2], hC[:, m, :], ALU.add).then_inc(freeC[bank], 1)

            def spikes(p, b, k):
                m, j = divmod(k, STEPS + 1)
                bank, use = USE_C["ffn2", m]
                y = bankC[bank][:, 0:T2]
                if j == 0:
                    if due(16 * p):
                        dve.wait_ge(s_out, 16 * p)
                    dve.wait_ge(fullC[bank], N_C[bank] * p + use + 1)
                    dve.tensor_scalar(cn[:, m, :], y, thresholds[0], None, ALU.is_gt).then_inc(s_cn, 1)
                elif j < STEPS:
                    dve.wait_ge(s_cn, 8 * p + 4 * m + j)
                    ins = dve.scalar_tensor_tensor(out=cn[:, m, :], in0=y, scalar=thresholds[j],
                                                   in1=cn[:, m, :], op0=ALU.is_gt, op1=ALU.add)
                    ins.then_inc(s_cn if j < STEPS - 1 else freeC[bank], 1)
                else:
                    dve.wait_ge(freeC[bank], N_C[bank] * (p + 1))
                    dve.scalar_tensor_tensor(out=cn[:, m, :], in0=cn[:, m, :], scalar=1.0 / STEPS, in1=h1[:, m, :],
                                             op0=ALU.mult, op1=ALU.add).then_inc(s_ow, 1)

            run(dve, {
                "stats1": lambda p, b, k: stats(p, bankA, fullA, N_A, st1, mv1, s_bn1, s_ag1),
                "apply1": lambda p, b, k: apply(p, bankA, freeA, mv1, nw1, nt, s_ln1),
                "silu_qk": silu_qk, "silu_v": silu_v, "split_v": split_v, "gate": gate, "q_hat": q_hat,
                "split_q": split_q, "score": score_max, "max_out": max_out, "p": part2, "o": heads_out,
                "wo_out": residual,
                "stats2": lambda p, b, k: stats(p, bankC, fullC, N_C, st2, mv2, s_bn2, s_ag2),
                "apply2": lambda p, b, k: apply(p, bankC, freeC, mv2, nw2, nt, s_ln2),
                "spikes": spikes})

        @block.gpsimd
        def _(pool):
            pool.wait_ge(s_const, 1)

            def newton(v, t, y, s, done, rounds):
                if due(done):
                    pool.wait_ge(s, done)
                    pool.nop(nofuse=True)
                pool.tensor_scalar(y.bitcast(I32), v.bitcast(I32), -0.5, RSQRT_SEED, ALU.mult, ALU.add).then_inc(s, 1)
                for k in range(rounds):
                    pool.wait_ge(s, done + (4 * k + 1))
                    pool.tensor_tensor(t, y, y, ALU.mult).then_inc(s, 1)
                    pool.wait_ge(s, done + (4 * k + 2))
                    pool.tensor_tensor(t, t, v, ALU.mult).then_inc(s, 1)
                    if due(done + (4 * k + 3)):
                        pool.wait_ge(s, done + (4 * k + 3))
                        pool.nop(nofuse=True)
                    pool.tensor_scalar(t, t, -0.5, 1.5, ALU.mult, ALU.add).then_inc(s, 1)
                    pool.wait_ge(s, done + (4 * k + 4))
                    pool.tensor_tensor(y, y, t, ALU.mult).then_inc(s, 1)

            def rstd(p, mv, nw, s_ag, s_ln):
                pool.wait_ge(s_ag, 4 * (p + 1))
                pool.nop(nofuse=True)
                pool.tensor_scalar(nw[:, 0, :], mv[:, :, 1], LN_EPS, None, ALU.add).then_inc(s_ln, 1)
                newton(nw[:, 0, :], nw[:, 2, :], nw[:, 1, :], s_ln, 14 * p + 1, 3)

            def norm_out(p, b, k):
                bank, use = USE_A["norm", 0]
                pool.wait_ge(freeA[bank], N_A[bank] * p + use + 1)
                newton(r2[:, :], nwr[:, 0, :], nwr[:, 1, :], s_rn, 12 * p, 2)
                pool.wait_ge(s_rn, 12 * p + 9)
                pool.nop(nofuse=True)
                pool.tensor_scalar(nwr[:, 0, :], nwr[:, 1, :], NORM_EPS, 0.0, ALU.mult, ALU.add).then_inc(s_rn, 1)
                pool.wait_ge(s_rn, 12 * p + 10)
                pool.nop(nofuse=True)
                pool.tensor_scalar(nwr[:, 1, :], nwr[:, 1, :], NORM_EPS, 1.0, ALU.mult, ALU.add).then_inc(s_rn, 1)

            def gate(p, b, k):
                pool.wait_ge(s_rec, p + 1)
                pool.tensor_tensor(g_sb[:, :], nwr[:, 0, :], r2[:, :], ALU.mult).then_inc(s_rn, 1)

            def split_v(p, b, t):
                r = ROWS[t % 2]
                pool.wait_ge(s_v2, 4 * p + t + 1)
                pool.tensor_tensor(vst[b][0:r, t, :, 2 * HD:3 * HD],
                                   tv[0:r, t, :].rearrange("p (h d) -> p h d", h=HEADS),
                                   vst[b][0:r, t, :, HD:2 * HD], ALU.subtract).then_inc(s_v3, 1)

            def split_q(p, b, c):
                pool.wait_ge(s_q2, 4 * p + c + 1)
                pool.tensor_tensor(parts[2][:, c, :], th[:, c, :], parts[1][:, c, :], ALU.subtract).then_inc(s_q3, 1)

            def max_out(p, b, img):
                pool.wait_ge(s_m2, 2 * p + img + 1)
                pool.tensor_tensor(mp[:, 2, :], mr[:, :], mp[:, 1, :], ALU.subtract).then_inc(s_m3, 1)

            def heads_out(p, b, n):
                if n % 4 != 3:
                    return
                g, img = (n % HEADS) // 4, n // HEADS
                bank, use = USE_O[n // 4]
                pool.wait_ge(freeO[bank], N_O[bank] * p + use + 1)
                for c in range(2):
                    r, t = ROWS[c], 2 * img + c
                    ins = pool.tensor_tensor(ot[0:r, t, 4 * g:4 * g + 4, :], ot[0:r, t, 4 * g:4 * g + 4, :],
                                             rd[0:r, t, 4 * g:4 * g + 4].unsqueeze(2).broadcast_to([r, 4, HD]),
                                             ALU.mult)
                ins.then_inc(s_ot, 1)

            def square_relu(p, b, f):
                bank, use = USE_C["ffn1", f]
                pool.wait_ge(freeC[bank], N_C[bank] * p + use + 1)
                pool.tensor_tensor(hs[:, f, :], rr[:, f % 2, :], rr[:, f % 2, :], ALU.mult).then_inc(s_hs, 1)

            run(pool, {
                "rstd1": lambda p, b, k: rstd(p, mv1, nw1, s_ag1, s_ln1),
                "norm_out": norm_out, "gate": gate, "split_v": split_v, "split_q": split_q, "max_out": max_out,
                "o": heads_out, "rstd2": lambda p, b, k: rstd(p, mv2, nw2, s_ag2, s_ln2),
                "ffn1_out": square_relu})


def kernel(x, cls_tok, L0_tok_W, L0_tok_b, L0_attn_Wq, L0_attn_Wk, L0_attn_Wv, L0_attn_Wo, L0_attn_q_scale,
           L0_attn_k_scale, L0_ffn_W_fc, L0_ffn_W_proj):
    import concourse.bacc as bacc
    from concourse.bass_utils import run_bass_kernel_spmd

    f = np.float32

    def features(w):
        w = np.asarray(w)
        return np.ascontiguousarray(w.T.reshape(w.shape[1] // P, P, w.shape[0]).transpose(1, 0, 2))

    n = np.asarray(x)
    patches = n.reshape(IMAGES, 3, 14, 16, 14, 16).transpose(0, 1, 2, 4, 3, 5).reshape(PAIRS, 2 * PATCHES, KC, P)
    x_t = np.ascontiguousarray(patches.transpose(0, 3, 2, 1)).reshape(PAIRS, P, KC * 2 * PATCHES)

    i, j = np.arange(P)[:, None], np.arange(P)[None, :]
    row_mask = np.zeros((P, P + TOK), f)
    row_mask[:, :P][j > i] = NEG
    row_mask[:, P:][np.arange(TOK)[None, :] > i + P] = NEG
    key_mask = np.zeros((P, P), f)
    key_mask[i > j] = NEG
    feature = np.arange(P)
    head_rows = np.zeros((P, 4, P), f)
    head_cols = np.zeros((2 * HEADS, 4, P), f)
    for c in range(4):
        head_rows[feature, c, 8 * c + feature % 8] = 1
        head_cols[8 * c + feature % 8, c, feature] = 1

    def per_feature(s):
        return np.ascontiguousarray(np.tile(np.asarray(s).reshape(DC, 8), (1, HD)).T)

    def feature_first(w):
        return np.asarray(w).reshape(DC, 8, HD, D).transpose(0, 2, 1, 3).reshape(D, D)

    arrays = {
        "x_t": x_t,
        "w_tok": features(L0_tok_W),
        "b_tok": np.ascontiguousarray(np.asarray(L0_tok_b).reshape(DC, P).T),
        "cls": np.ascontiguousarray(np.asarray(cls_tok).reshape(DC, P).T),
        "w_qk": features(np.concatenate([feature_first(L0_attn_Wq), feature_first(L0_attn_Wk)], 0)),
        "w_v": features(L0_attn_Wv),
        "w_o": features(L0_attn_Wo),
        "w_fc": features(L0_ffn_W_fc),
        "w_proj": features(L0_ffn_W_proj),
        "q_scale": per_feature(L0_attn_q_scale),
        "k_scale": per_feature(L0_attn_k_scale),
        "eye": np.eye(P, dtype=f),
        "row_mask": row_mask,
        "key_mask": key_mask,
        "head_rows": head_rows,
        "head_cols": head_cols,
    }
    nc = bacc.Bacc("TRN2", target_bir_lowering=False, num_devices=1)
    args = [nc.dram_tensor(name, a.shape, mybir.dt.from_np(a.dtype), kind="ExternalInput").ap()
            for name, a in arrays.items()]
    out_t = nc.dram_tensor("out_t", (PAIRS, P, DC * T2), F32, kind="ExternalOutput").ap()
    program(nc, *args, out_t)
    r = run_bass_kernel_spmd(nc, [arrays], core_ids=[0])
    got = r.results[0]["out_t"].reshape(PAIRS, P, DC, 2, TOK)
    return np.ascontiguousarray(got.transpose(0, 3, 4, 2, 1)).reshape(IMAGES, TOK, D)
```

```python
from contextlib import ExitStack

import numpy as np

import concourse.bass as bass
from concourse import mybir

F32 = mybir.dt.float32
F32R = mybir.dt.float32r
BF16 = mybir.dt.bfloat16
F16 = mybir.dt.float16
I32 = mybir.dt.int32
ALU = mybir.AluOpType
ACT = mybir.ActivationFunctionType
AX = mybir.AxisListType

IMAGES = 64
PAIRS = IMAGES // 2
PATCHES = 196
TOK = PATCHES + 1
T2 = 2 * TOK
D = 256
KIN = 768
HEADS = 16
HD = D // HEADS
FF = 4 * D
P = 128
KC, DC, FC = KIN // P, D // P, FF // P
TAIL = TOK - P
ROWS = (P, TAIL)
VW = 50
NEG = -1e30
LN_EPS = 1e-5
NORM_EPS = 1e-6
RSQRT_SEED = float(0x5F3759DF)
Q_PARTS = (0, 0, 1, 1, 0, 2)
K_PARTS = (0, 1, 0, 1, 2, 0)
KROWS = HD * len(Q_PARTS)
STEPS, BETA, THRESHOLD = 5, 0.9, 1.0

USE_A = {("embed", 0): (0, 0), ("embed", 1): (1, 0), ("turn", 0): (0, 1), ("turn", 1): (1, 1),
         ("back", 0): (0, 2), ("back", 1): (1, 2), ("qk", 0): (0, 3), ("qk", 1): (1, 3),
         ("qk", 2): (0, 4), ("qk", 3): (1, 4), ("norm", 0): (0, 5), ("g", 0): (1, 5), ("g", 1): (0, 6),
         ("g", 2): (1, 6), ("g", 3): (0, 7), ("v", 0): (1, 7), ("v", 1): (0, 8), ("v", 2): (1, 8), ("v", 3): (0, 9)}
N_A = (10, 9)
USE_C = {("wo", 0): (0, 0), ("wo", 1): (1, 0), ("turn", 0): (0, 1), ("turn", 1): (1, 1),
         ("back", 0): (0, 2), ("back", 1): (1, 2), ("ffn2", 0): (0, 7), ("ffn2", 1): (1, 7)}
USE_C.update({("ffn1", f): (f % 2, 3 + f // 2) for f in range(FC)})
N_C = (8, 8)
N_S = 2 * (HEADS + 1)
N_ST = 2 * HEADS
USE_O = {g: (g % 2, g // 2 + (g > 3) * (g % 2)) for g in range(8)}
USE_OT = (2, 5)
N_O = (4, 6)


def place(h):
    return 2 * (h % 8) + h // 8


def spike_thresholds():
    f = np.float32

    def count(y):
        mem, n = f(0), 0
        for _ in range(STEPS):
            mem = f(f(f(BETA) * mem) + y) - f(mem - f(THRESHOLD) > 0)
            n += int(mem - f(THRESHOLD) > 0)
        return n

    out = []
    for want in range(1, STEPS + 1):
        lo, hi = int(f(0.01).view(np.int32)), int(f(2.0).view(np.int32))
        while hi - lo > 1:
            mid = (lo + hi) // 2
            if count(np.int32(mid).view(np.float32)) >= want:
                hi = mid
            else:
                lo = mid
        out.append(float(np.int32(lo).view(np.float32)))
    return out


SLOTS = 2 * HEADS
STEPS_AT = {
    "load_x": (-56.99,),
    "embed_mm": (-34.59, -33.26, -32.12, -31.22, -30.55, -30.07),
    "embed_out": (-30.61, -30.25),
    "turn1_mm": (-29.42, -29.26),
    "stats1": (-29.72,),
    "rstd1": (-29.62,),
    "apply1": (-25.62, -25.13, -23.85, -23.82),
    "back1_mm": (-22.76, -22.07),
    "back1_out": (-22.94, -22.58),
    "qk_mm": (-20.94, -20.24, -19.79, -19.12),
    "silu_qk": (-20.75, -19.99, -19.66, -19.09),
    "square": (-19.88, -19.60, -18.74, -18.13),
    "norm_mm": (-17.20,),
    "norm_out": (-17.32,),
    "over_norm": (-17.34, -16.93, -16.41, -15.87, -14.34, -13.87, -13.52, -13.19, -13.01, -12.59, -12.04),
    "gate": (-10.00,),
    "g_mm": (-8.79, -8.51, -8.30, -8.07),
    "q_hat": (-9.06, -8.98, -8.83, -8.39),
    "split_q": (-8.56, -8.51, -8.38, -7.52),
    "split_q2": (-8.30, -8.09, -7.47, -6.03),
    "restack": (-13.63,),
    "v_mm": (-7.73, -7.12, -6.18, -5.44),
    "silu_v": (-8.29, -6.74, -5.74, -4.79),
    "split_v": (-6.26, -1.89, -1.53, -0.99),
    "split_v2": (-3.58, -1.36, -0.53, 10.99),
    "keep_h": (26.18,),
    "ot_mm": (42.17, 58.08),
    "ot_out": (43.95, 58.45),
    "wo_mm": (59.94, 60.87),
    "wo_out": (60.92, 61.13),
    "turn2_mm": (62.04, 62.35),
    "stats2": (62.31,),
    "rstd2": (62.84,),
    "apply2": (65.52, 65.59, 66.11, 66.14),
    "back2_mm": (67.08, 67.09),
    "back2_out": (66.80, 67.21),
    "ffn1_mm": (67.61, 68.85, 69.47, 71.02, 71.85, 72.70, 73.80, 77.73),
    "ffn1_out": (68.17, 69.81, 70.44, 72.05, 72.21, 73.80, 73.93, 78.18),
    "ffn2_mm": (80.05, 80.45, 81.74, 81.96, 83.05, 85.04, 87.13, 88.81),
    "spikes": (81.75, 82.19, 84.03, 85.75, 86.20, 86.77, 88.93, 89.97, 90.29, 91.04, 91.16, 91.35),
    "store": (86.60,),
}
HEAD_AT = {"score": 2.14, "st": 22.34, "p": 23.32, "pv": 24.98, "o": 25.30}
MAX_AT = {"max_mm": 17.76, "max_out": 17.48, "max_out2": 18.24}


def order():
    at = [(x, step, k) for step, places in STEPS_AT.items() for k, x in enumerate(places)]
    at += [(x + n, step, n) for step, x in HEAD_AT.items() for n in range(SLOTS)]
    at += [(x + HEADS * img, step, img) for step, x in MAX_AT.items() for img in range(2)]
    return [(step, k, -int(x // SLOTS)) for x, step, k in sorted(at, key=lambda a: (a[0] % SLOTS, a[1], a[2]))]


ORDER = order()
LOOP_FROM = 4


def program(nc, x_t, w_tok, b_tok, cls, w_qk, w_v, w_o, w_fc, w_proj, q_scale, k_scale,
            eye, row_mask, key_mask, head_rows, head_cols, out_t):
    thresholds = spike_thresholds()
    with ExitStack() as ctx:
        def sb(name, shape, dt=F32):
            return ctx.enter_context(nc.sbuf_tensor(name, shape, dt))

        def psum(name):
            return ctx.enter_context(nc.psum_tensor(name, [P, 512], F32))

        def sem(name):
            return ctx.enter_context(nc.semaphore(name))

        wtok = sb("wtok", [P, KC, D])
        btok = sb("btok", [P, DC])
        clsT = sb("clsT", [P, DC])
        wqk = sb("wqk", [P, DC, 2 * D])
        wv = sb("wv", [P, DC, D])
        wo = sb("wo", [P, DC, D])
        wfc = sb("wfc", [P, DC, FF])
        wproj = sb("wproj", [P, FC, D])
        qsc = sb("qsc", [P, DC])
        ksc = sb("ksc", [P, DC])
        sc = sb("sc", [P, 4])
        eyef = sb("eyef", [P, P])
        eyeb = sb("eyeb", [P, P], BF16)
        rowmask = sb("rowmask", [P, P + TOK])
        keymask = sb("keymask", [P, P], BF16)
        hrows = sb("hrows", [P, 4, P], F32R)
        hcols = sb("hcols", [2 * HEADS, 4, P], F32R)

        x_sb = sb("x_sb", [P, KC, 2 * PATCHES])
        hA = [sb(f"hA{b}", [P, DC, 2, TOK]) for b in range(2)]
        hC = sb("hC", [P, DC, T2])
        st1 = sb("st1", [P, 4, 6])
        mv1 = sb("mv1", [P, 4, 2])
        nw1 = sb("nw1", [P, 3, 4])
        nt = sb("nt", [P, 4, D])
        lnT = sb("lnT", [P, DC, T2])
        th = sb("th", [P, 4, T2])
        s2 = sb("s2", [P, 4, T2])
        sq = sb("sq", [P, 4, T2], F32R)
        r2 = sb("r2", [2 * HEADS, T2])
        nwr = sb("nwr", [2 * HEADS, 2, T2])
        g_sb = sb("g_sb", [2 * HEADS, T2], F32R)
        parts = [sb(f"part{j}", [P, 4, T2], BF16) for j in range(3)]
        tv = sb("tv", [P, 4, D])
        v2 = sb("v2", [P, 4, D])
        qst = [sb(f"qst{b}", [KROWS + 3, HEADS, T2], BF16) for b in range(2)]
        kst = [sb(f"kst{b}", [KROWS + 3, HEADS * T2 + 64], BF16) for b in range(2)]
        vst = [sb(f"vst{b}", [P, 4, HEADS, VW], BF16) for b in range(2)]
        mx = sb("mx", [P, 2, 2, HEADS])
        mr = sb("mr", [HEADS, TOK])
        mp = sb("mp", [HEADS, 3, TOK], BF16)
        p32 = sb("p32", [P, 2, TOK + TAIL])
        p1 = sb("p1", [P, 2, TOK + TAIL], F16)
        p2 = sb("p2", [P, 2, TOK + TAIL], F16)
        rd = sb("rd", [P, 4, HEADS])
        ot = sb("ot", [P, 4, HEADS, HD])
        oT = sb("oT", [P, DC, 2, TOK])
        h1 = sb("h1", [P, DC, T2])
        st2 = sb("st2", [P, 4, 6])
        mv2 = sb("mv2", [P, 4, 2])
        nw2 = sb("nw2", [P, 3, 4])
        l2T = sb("l2T", [P, DC, T2])
        rr = sb("rr", [P, 2, T2])
        hs = sb("hs", [P, FC, T2])
        cn = sb("cn", [P, DC, T2])
        hrowsf = hs[:, 0:4, 0:P]
        hcolsf = hs[0:2 * HEADS, 4:8, 0:P]
        keymaskf = hs[:, 0, P:2 * P]

        bankA = [psum("bankA0"), psum("bankA1")]
        bankC = [psum("bankC0"), psum("bankC1")]
        bankS, bankST, bankO = psum("bankS"), psum("bankST"), [psum("bankO0"), psum("bankO1")]

        fullA, freeA = [sem("fullA0"), sem("fullA1")], [sem("freeA0"), sem("freeA1")]
        fullC, freeC = [sem("fullC0"), sem("fullC1")], [sem("freeC0"), sem("freeC1")]
        fullS, freeS = sem("fullS"), sem("freeS")
        fullST, freeST = sem("fullST"), sem("freeST")
        freeO = [sem("freeO0"), sem("freeO1")]
        full_ot = sem("heads_turned")
        s_we, s_wc, s_w = sem("embedding_in"), sem("constants_in"), sem("weights_in")
        s_const = sem("constants_ready")
        s_x = sem("x_in")
        s_hc = sem("h_kept")
        s_bn1, s_ag1, s_ln1 = sem("bn_stats_1"), sem("bn_aggr_1"), sem("rstd_1_steps")
        s_bn2, s_ag2, s_ln2 = sem("bn_stats_2"), sem("bn_aggr_2"), sem("rstd_2_steps")
        s_th, s_sq = sem("tanh_qk"), sem("squares")
        s_rn, s_rec = sem("norm_steps"), sem("norm_reciprocal")
        s_q1, s_r1, s_q2, s_q3 = sem("qk_part1"), sem("qk_rest"), sem("qk_part2"), sem("qk_part3")
        s_tv, s_v1, s_rv, s_v2, s_v3 = sem("tanh_v"), sem("v_part1"), sem("v_rest"), sem("v_part2"), sem("v_part3")
        s_stack = sem("stack_in")
        s_m1, s_m2, s_m3, s_mrow = sem("max_part1"), sem("max_part2"), sem("max_part3"), sem("max_rows_in")
        s_p1, s_p2, s_pv = sem("p_part1"), sem("p_part2"), sem("pv_done")
        s_ot = sem("heads_divided")
        s_hs = sem("ffn_hidden")
        s_cn, s_ow, s_out = sem("count_steps"), sem("out_ready"), sem("out_stored")

        def x_of(p):
            return x_t[p].rearrange("p (k n) -> p k n", k=KC)

        embedding = [(wtok[:, :, :], w_tok), (x_sb[:, :, :], x_of(0)), (btok[:, :], b_tok)]
        constants = [(eyef[:, :], eye), (clsT[:, :], cls), (hrowsf, head_rows), (hcolsf, head_cols),
                     (keymaskf, key_mask), (qsc[:, :], q_scale), (ksc[:, :], k_scale)]
        weights = [(wqk[:, :, :], w_qk), (wv[:, :, :], w_v), (rowmask[:, :], row_mask), (wo[:, :, :], w_o),
                   (wfc[:, :, :], w_fc), (wproj[:, :, :], w_proj)]

        block = ctx.enter_context(nc.Block())

        def due(count):
            return not isinstance(count, int) or count > 0

        def first(p):
            return isinstance(p, int) and p == 0

        def run(eng, mine):
            def peeled(i):
                for step, k, lag in ORDER:
                    if step in mine and 0 <= i + lag < PAIRS:
                        mine[step](i + lag, (i + lag) % 2, k)

            for i in range(-2, LOOP_FROM):
                peeled(i)
            with eng.Fori(LOOP_FROM, PAIRS - 3, 2) as i:
                for u in range(2):
                    for step, k, lag in ORDER:
                        if step in mine:
                            mine[step](i + (u + lag), (LOOP_FROM + u + lag) % 2, k)
            for i in range(PAIRS - 2, PAIRS + 2):
                peeled(i)

        @block.sync
        def _(sp):
            for dst, src in embedding:
                sp.dma_start(dst, src).then_inc(s_we, 16)
            for dst, src in constants:
                sp.dma_start(dst, src).then_inc(s_wc, 16)
            for dst, src in weights:
                sp.dma_start(dst, src).then_inc(s_w, 16)

            def load_x(p, b, k):
                if first(p):
                    return
                if due(N_A[1] * (p - 1) + 1):
                    sp.wait_ge(fullA[1], N_A[1] * (p - 1) + 1)
                sp.dma_start(x_sb[:, :, :], x_of(p)).then_inc(s_x, 16)

            def keep_h(p, b, k):
                sp.wait_ge(freeA[0], N_A[0] * p + 1)
                sp.wait_ge(freeA[1], N_A[1] * p + 1)
                if due(N_C[0] * (p - 1) + 1):
                    sp.wait_ge(freeC[0], N_C[0] * (p - 1) + 1)
                if due(N_C[1] * (p - 1) + 1):
                    sp.wait_ge(freeC[1], N_C[1] * (p - 1) + 1)
                sp.dma_start(hC[:, :, :], hA[b][:, :, :, :].rearrange("p c i n -> p c (i n)")).then_inc(s_hc, 16)

            def restack(p, b, k):
                if due(N_ST * (p - 1)):
                    sp.wait_ge(fullST, N_ST * (p - 1))
                    sp.nop(nofuse=True)
                sp.wait_ge(s_q1, 4 * (p + 1))
                sp.wait_ge(s_q2, 4 * (p + 1))
                sp.wait_ge(s_q3, 4 * (p + 1))
                for j in range(len(Q_PARTS)):
                    rows = slice(HD * j, HD * (j + 1))
                    sp.dma_start(qst[b][rows, :, :], parts[Q_PARTS[j]][:, 0:2, :]).then_inc(s_stack, 16)
                    sp.dma_start(kst[b][rows, 0:HEADS * T2], parts[K_PARTS[j]][:, 2:4, :]).then_inc(s_stack, 16)

            def max_rows(p, b, img):
                sp.wait_ge(s_m3, 2 * p + img + 1)
                for j in range(3):
                    sp.dma_start(qst[b][KROWS + j:KROWS + j + 1, :, img * TOK:(img + 1) * TOK],
                                 mp[:, j, :]).then_inc(s_mrow, 16)

            def store(p, b, k):
                sp.wait_ge(s_ow, 2 * (p + 1))
                sp.dma_start(out_t[p].rearrange("p (c n) -> p c n", c=DC), cn[:, :, :]).then_inc(s_out, 16)

            run(sp, {"load_x": load_x, "keep_h": keep_h, "restack": restack, "max_out2": max_rows, "store": store})
            sp.wait_ge(s_out, 16 * PAIRS)

        @block.tensor
        def _(pe):
            pe.wait_ge(s_we, 16 * len(embedding))

            def embed(p, b, third):
                m, third = divmod(third, 3)
                bank, use = USE_A["embed", m]
                if third == 0:
                    if not first(p):
                        pe.wait_ge(s_x, 16 * p)
                    if due(N_A[bank] * p + use):
                        pe.wait_ge(freeA[bank], N_A[bank] * p + use)
                for k in range(2 * third, 2 * third + 2):
                    mm = pe.matmul(bankA[bank][:, 0:2 * PATCHES], wtok[:, k, m * P:(m + 1) * P], x_sb[:, k, :],
                                   start=(k == 0), stop=(k == KC - 1))
                if third == 2:
                    mm.then_inc(fullA[bank], 1)

            def turn(p, img, src, banks, full, free, per, uses):
                if first(p):
                    pe.wait_ge(s_const, 1)
                bank, use = uses["turn", img]
                pe.wait_ge(free[0], per[0] * p + 1)
                pe.wait_ge(free[1], per[1] * p + 1)
                for c in range(2):
                    for m in range(DC):
                        n0 = c * P
                        mm = pe.transpose(banks[bank][0:ROWS[c], c * D + m * P:c * D + (m + 1) * P],
                                          src(m, img, n0, n0 + ROWS[c]), eyef[:, :])
                mm.then_inc(full[bank], 1)

            def back(p, m, src, banks, full, free, per, uses):
                bank, use = uses["back", m]
                pe.wait_ge(free[0], per[0] * p + 2)
                pe.wait_ge(free[1], per[1] * p + 2)
                for t in range(4):
                    n0 = (t // 2) * TOK + (t % 2) * P
                    r = ROWS[t % 2]
                    mm = pe.transpose(banks[bank][:, n0:n0 + r], src[0:r, t, m * P:(m + 1) * P], eyef[0:r, 0:r])
                mm.then_inc(full[bank], 1)

            def qk(p, b, c):
                bank, use = USE_A["qk", c]
                pe.wait_ge(freeA[1 - bank], N_A[1 - bank] * p + 3)
                if due(N_A[bank] * p + use):
                    pe.wait_ge(freeA[bank], N_A[bank] * p + use)
                if first(p):
                    pe.wait_ge(s_w, 16 * len(weights))
                for k in range(DC):
                    mm = pe.matmul(bankA[bank][:, 0:T2], wqk[:, k, c * P:(c + 1) * P], lnT[:, k, :],
                                   start=(k == 0), stop=(k == DC - 1))
                mm.then_inc(fullA[bank], 1)

            def v(p, b, t):
                bank, use = USE_A["v", t]
                n0, r = (t // 2) * TOK + (t % 2) * P, ROWS[t % 2]
                if due(N_A[bank] * p + use):
                    pe.wait_ge(freeA[bank], N_A[bank] * p + use)
                for k in range(DC):
                    mm = pe.matmul(bankA[bank][0:r, 0:D], lnT[:, k, n0:n0 + r], wv[:, k, :],
                                   start=(k == 0), stop=(k == DC - 1))
                mm.then_inc(fullA[bank], 1)

            def norm(p, b, _k):
                bank, use = USE_A["norm", 0]
                pe.wait_ge(s_sq, 4 * (p + 1))
                if due(N_A[bank] * p + use):
                    pe.wait_ge(freeA[bank], N_A[bank] * p + use)
                for c in range(4):
                    mm = pe.matmul(bankA[bank][:, 0:T2], hrows[:, c, :], sq[:, c, :], start=(c == 0), stop=(c == 3))
                mm.then_inc(fullA[bank], 1)

            def g(p, b, c):
                bank, use = USE_A["g", c]
                pe.wait_ge(s_rn, 12 * (p + 1))
                if due(N_A[bank] * p + use):
                    pe.wait_ge(freeA[bank], N_A[bank] * p + use)
                pe.matmul(bankA[bank][:, 0:T2], hcols[:, c, :], g_sb[:, :], start=True,
                          stop=True).then_inc(fullA[bank], 1)

            def score(p, b, s):
                img, h = s // HEADS, s % HEADS
                if s == 0:
                    pe.wait_ge(s_stack, 16 * 12 * (p + 1))
                if due(N_S * p + img * (HEADS + 1) + h):
                    pe.wait_ge(freeS, N_S * p + img * (HEADS + 1) + h)
                at = place(h)
                q0, k0 = img * TOK, at * T2 + img * TOK
                pe.matmul(bankS[:, 0:P], qst[b][0:KROWS, at, q0:q0 + P], kst[b][0:KROWS, k0:k0 + P],
                          start=True, stop=True)
                pe.matmul(bankS[0:TAIL, P:P + TOK], qst[b][0:KROWS, at, q0 + P:q0 + TOK],
                          kst[b][0:KROWS, k0:k0 + TOK], start=True, stop=True).then_inc(fullS, 1)

            def max_turn(p, b, img):
                use = N_S * p + img * (HEADS + 1) + HEADS
                if due(use):
                    pe.wait_ge(freeS, use)
                pe.transpose(bankS[0:HEADS, 0:P], mx[:, img, 0, :], eyef[:, :])
                pe.transpose(bankS[0:HEADS, P:TOK], mx[0:TAIL, img, 1, :], eyef[0:TAIL, 0:TAIL]).then_inc(fullS, 1)

            def st(p, b, n):
                img, h = n // HEADS, n % HEADS
                if h == 0:
                    if due(16 * 3 * (2 * p + img + 1)):
                        pe.wait_ge(s_mrow, 16 * 3 * (2 * p + img + 1))
                if due(N_ST * p + n):
                    pe.wait_ge(freeST, N_ST * p + n)
                at = place(h)
                q0, k0 = img * TOK, at * T2 + img * TOK
                pe.matmul(bankST[:, 0:TOK], kst[b][:, k0:k0 + P], qst[b][:, at, q0:q0 + TOK], start=True, stop=False,
                          skip_group_check=True)
                pe.matmul(bankST[:, 0:P], eyeb[:, :], keymask[:, :], start=False, stop=True, skip_group_check=True)
                pe.matmul(bankST[:, TOK:TOK + TAIL], kst[b][:, k0 + P:k0 + 2 * P], qst[b][:, at, q0 + P:q0 + TOK],
                          start=True, stop=False, skip_group_check=True)
                pe.matmul(bankST[:, TOK:TOK + TAIL], eyeb[:, :], keymask[:, 0:TAIL], start=False, stop=True,
                          skip_group_check=True).then_inc(fullST, 1)

            def pv(p, b, n):
                img, h = n // HEADS, n % HEADS
                if n == 0:
                    pe.wait_ge(s_v2, 4 * (p + 1))
                    pe.wait_ge(s_v3, 4 * (p + 1))
                pe.wait_ge(s_p2, N_ST * p + n + 1)
                bank, use = USE_O[n // 4]
                if n % 4 == 0 and due(N_O[bank] * p + use):
                    pe.wait_ge(freeO[bank], N_O[bank] * p + use)
                w, hh, t = n % 2, h % 4, 2 * img
                o0 = bankO[bank][:, hh * VW:(hh + 1) * VW]
                o1 = bankO[bank][0:TAIL, (4 + hh) * VW:(5 + hh) * VW]
                pe.matmul(o0, p1[:, w, 0:P], vst[b][:, t, h, :], start=True, stop=False, skip_group_check=True)
                pe.matmul(o0, p2[:, w, 0:P], vst[b][:, t, h, :], start=False, stop=True, skip_group_check=True)
                pe.matmul(o1, p1[:, w, P:TOK], vst[b][:, t, h, :], start=True, stop=False, skip_group_check=True)
                pe.matmul(o1, p2[:, w, P:TOK], vst[b][:, t, h, :], start=False, stop=False, skip_group_check=True)
                pe.matmul(o1, p1[0:TAIL, w, TOK:], vst[b][0:TAIL, t + 1, h, :], start=False, stop=False,
                          skip_group_check=True)
                pe.matmul(o1, p2[0:TAIL, w, TOK:], vst[b][0:TAIL, t + 1, h, :], start=False, stop=True,
                          skip_group_check=True).then_inc(s_pv, 1)

            def ot_turn(p, b, img):
                pe.wait_ge(s_ot, 8 * p + 4 * (img + 1))
                pe.wait_ge(freeO[1], N_O[1] * p + USE_OT[img])
                for m in range(DC):
                    for c in range(2):
                        r = ROWS[c]
                        mm = pe.transpose(bankO[1][:, m * TOK + c * P:m * TOK + c * P + r],
                                          ot[0:r, 2 * img + c, 8 * m:8 * (m + 1), :].rearrange("p h d -> p (h d)"),
                                          eyef[0:r, 0:r])
                mm.then_inc(full_ot, 1)

            def project(p, b, m):
                bank, use = USE_C["wo", m]
                pe.wait_ge(freeO[1], N_O[1] * (p + 1))
                if due(N_C[bank] * p + use):
                    pe.wait_ge(freeC[bank], N_C[bank] * p + use)
                for k in range(DC):
                    mm = pe.matmul(bankC[bank][:, 0:T2], wo[:, k, m * P:(m + 1) * P],
                                   oT[:, k, :, :].rearrange("p i n -> p (i n)"), start=(k == 0), stop=(k == DC - 1))
                mm.then_inc(fullC[bank], 1)

            def ffn1(p, b, f):
                bank, use = USE_C["ffn1", f]
                pe.wait_ge(freeC[1 - bank], N_C[1 - bank] * p + 3)
                if due(N_C[bank] * p + use):
                    pe.wait_ge(freeC[bank], N_C[bank] * p + use)
                for k in range(DC):
                    mm = pe.matmul(bankC[bank][:, 0:T2], wfc[:, k, f * P:(f + 1) * P], l2T[:, k, :],
                                   start=(k == 0), stop=(k == DC - 1))
                mm.then_inc(fullC[bank], 1)

            def ffn2(p, b, quarter):
                m, quarter = divmod(quarter, 4)
                bank, use = USE_C["ffn2", m]
                if quarter == 0:
                    pe.wait_ge(s_hs, FC * (p + 1))
                    pe.wait_ge(freeC[bank], N_C[bank] * p + use)
                for f in range(2 * quarter, 2 * quarter + 2):
                    mm = pe.matmul(bankC[bank][:, 0:T2], wproj[:, f, m * P:(m + 1) * P], hs[:, f, :],
                                   start=(f == 0), stop=(f == FC - 1))
                if quarter == 3:
                    mm.then_inc(fullC[bank], 1)

            run(pe, {
                "embed_mm": embed,
                "turn1_mm": lambda p, b, k: turn(p, k, lambda m, i, a, e: hA[b][:, m, i, a:e],
                                                 bankA, fullA, freeA, N_A, USE_A),
                "back1_mm": lambda p, b, k: back(p, k, nt, bankA, fullA, freeA, N_A, USE_A),
                "qk_mm": qk, "v_mm": v, "norm_mm": norm, "g_mm": g,
                "score": score, "max_mm": max_turn, "st": st, "pv": pv, "ot_mm": ot_turn, "wo_mm": project,
                "turn2_mm": lambda p, b, k: turn(p, k, lambda m, i, a, e: h1[:, m, i * TOK + a:i * TOK + e],
                                                 bankC, fullC, freeC, N_C, USE_C),
                "back2_mm": lambda p, b, k: back(p, k, nt, bankC, fullC, freeC, N_C, USE_C),
                "ffn1_mm": ffn1, "ffn2_mm": ffn2})

        @block.scalar
        def _(act):
            act.wait_ge(s_we, 16 * len(embedding))

            def embed_out(p, b, m):
                bank, use = USE_A["embed", m]
                if due(16 * (p - 1)):
                    act.wait_ge(s_hc, 16 * (p - 1))
                act.wait_ge(fullA[bank], N_A[bank] * p + use + 1)
                act.activation(hA[b][:, m, :, 1:TOK], bankA[bank][:, 0:2 * PATCHES].rearrange("p (i n) -> p i n", i=2),
                               ACT.Identity, bias=btok[:, m:m + 1]).then_inc(freeA[bank], 1)

            def apply(p, t, banks, free, nw, s_ln):
                img, r = t // 2, ROWS[t % 2]
                act.wait_ge(s_ln, 16 * (p + 1))
                ins = act.activation(nt[0:r, t, :], banks[img][0:r, (t % 2) * D:(t % 2 + 1) * D], ACT.Identity,
                                     bias=nw[0:r, 2, t:t + 1], scale=nw[0:r, 1, t:t + 1])
                if t % 2:
                    ins.then_inc(free[img], 1)

            def back_out(p, m, dst, banks, full, free, per, uses):
                bank, use = uses["back", m]
                act.wait_ge(full[bank], per[bank] * p + use + 1)
                act.activation(dst[:, m, :], banks[bank][:, 0:T2], ACT.Copy).then_inc(free[bank], 1)

            def tanh_qk(p, b, c):
                bank, use = USE_A["qk", c]
                if due(4 * p):
                    act.wait_ge(s_q3, 4 * p)
                act.wait_ge(fullA[bank], N_A[bank] * p + use + 1)
                act.activation(th[:, c, :], bankA[bank][:, 0:T2], ACT.Tanh, scale=0.5).then_inc(s_th, 1)

            def square(p, b, c):
                bank, use = USE_A["qk", c]
                act.wait_ge(freeA[bank], N_A[bank] * p + use + 1)
                act.activation(sq[:, c, :], s2[:, c, :], ACT.Square, scale=0.5).then_inc(s_sq, 1)

            def norm_out(p, b, k):
                bank, use = USE_A["norm", 0]
                if due(12 * p):
                    act.wait_ge(s_rn, 12 * p)
                act.wait_ge(fullA[bank], N_A[bank] * p + use + 1)
                act.activation(r2[:, :], bankA[bank][0:2 * HEADS, 0:T2], ACT.Copy).then_inc(freeA[bank], 1)

            def tanh_v(p, b, t):
                bank, use = USE_A["v", t]
                r = ROWS[t % 2]
                if due(4 * p):
                    act.wait_ge(s_v3, 4 * p)
                act.wait_ge(fullA[bank], N_A[bank] * p + use + 1)
                act.activation(tv[0:r, t, :], bankA[bank][0:r, 0:D], ACT.Tanh, scale=0.5).then_inc(s_tv, 1)

            def split_v(p, b, t):
                bank, use = USE_A["v", t]
                r = ROWS[t % 2]
                if due(N_ST * (p - 1)):
                    act.wait_ge(s_pv, N_ST * (p - 1))
                act.wait_ge(freeA[bank], N_A[bank] * p + use + 1)
                act.activation(vst[b][0:r, t, :, 0:HD], v2[0:r, t, :].rearrange("p (h d) -> p h d", h=HEADS),
                               ACT.Copy).then_inc(s_v1, 1)

            def split_v2(p, b, t):
                r = ROWS[t % 2]
                act.wait_ge(s_rv, 4 * p + t + 1)
                act.activation(vst[b][0:r, t, :, HD:2 * HD], tv[0:r, t, :].rearrange("p (h d) -> p h d", h=HEADS),
                               ACT.Copy).then_inc(s_v2, 1)

            def split_q(p, b, c):
                bank, use = USE_A["g", c]
                if first(p):
                    act.wait_ge(s_const, 1)
                if due(16 * 12 * p):
                    act.wait_ge(s_stack, 16 * 12 * p)
                act.wait_ge(freeA[bank], N_A[bank] * p + use + 1)
                act.activation(parts[0][:, c, :], th[:, c, :], ACT.Copy, scale=sc[:, c:c + 1]).then_inc(s_q1, 1)

            def split_q2(p, b, c):
                act.wait_ge(s_r1, 4 * p + c + 1)
                act.activation(parts[1][:, c, :], th[:, c, :], ACT.Copy).then_inc(s_q2, 1)

            def max_out(p, b, img):
                if due(16 * 3 * (2 * p + img)):
                    act.wait_ge(s_mrow, 16 * 3 * (2 * p + img))
                act.wait_ge(fullS, N_S * p + img * (HEADS + 1) + HEADS + 1)
                act.activation(mp[:, 0, :], bankS[0:HEADS, 0:TOK], ACT.Copy).then_inc(s_m1, 1)

            def max_out2(p, b, img):
                act.wait_ge(freeS, N_S * p + (img + 1) * (HEADS + 1))
                act.activation(mp[:, 1, :], mr[:, :], ACT.Copy).then_inc(s_m2, 1)

            def exp(p, b, n):
                if due(N_ST * p + n - 1):
                    act.wait_ge(s_p2, N_ST * p + n - 1)
                act.wait_ge(fullST, N_ST * p + n + 1)
                act.activation(p32[:, n % 2, :], bankST[:, 0:TOK + TAIL], ACT.Exp).then_inc(freeST, 1)

            def part1(p, b, n):
                if due(N_ST * p + n - 1):
                    act.wait_ge(s_pv, N_ST * p + n - 1)
                act.wait_ge(freeST, N_ST * p + n + 1)
                act.activation(p1[:, n % 2, :], p32[:, n % 2, :], ACT.Copy).then_inc(s_p1, 1)

            def ot_out(p, b, img):
                act.wait_ge(full_ot, 2 * p + img + 1)
                act.activation(oT[:, :, img, :], bankO[1][:, 0:2 * TOK].rearrange("p (m n) -> p m n", m=DC),
                               ACT.Copy).then_inc(freeO[1], 1)

            def relu(p, b, f):
                bank, use = USE_C["ffn1", f]
                if due(FC * p + f - 1):
                    act.wait_ge(s_hs, FC * p + f - 1)
                act.wait_ge(fullC[bank], N_C[bank] * p + use + 1)
                act.activation(rr[:, f % 2, :], bankC[bank][:, 0:T2], ACT.Relu).then_inc(freeC[bank], 1)

            run(act, {
                "apply1": lambda p, b, t: apply(p, t, bankA, freeA, nw1, s_ln1),
                "apply2": lambda p, b, t: apply(p, t, bankC, freeC, nw2, s_ln2),
                "embed_out": embed_out,
                "back1_out": lambda p, b, k: back_out(p, k, lnT, bankA, fullA, freeA, N_A, USE_A),
                "silu_qk": tanh_qk, "square": square, "norm_out": norm_out, "silu_v": tanh_v, "split_v": split_v,
                "split_v2": split_v2, "split_q": split_q, "split_q2": split_q2, "max_out": max_out,
                "max_out2": max_out2, "st": exp, "p": part1, "ot_out": ot_out,
                "back2_out": lambda p, b, k: back_out(p, k, l2T, bankC, fullC, freeC, N_C, USE_C),
                "ffn1_out": relu})

        @block.vector
        def _(dve):
            for b in range(2):
                dve.memset(kst[b][:, HEADS * T2:], 0.0)
                dve.memset(kst[b][KROWS:KROWS + 3, 0:HEADS * T2], -1.0)
                dve.memset(vst[b][:, :, :, 3 * HD:3 * HD + 1], 2.0)
                dve.memset(vst[b][:, :, :, 3 * HD + 1:], 0.0)
            dve.memset(mv1[:, :, :], 1.0)
            dve.memset(mv2[:, :, :], 1.0)
            dve.wait_ge(s_wc, 16 * len(constants))
            dve.tensor_copy(eyeb[:, :], eyef[:, :])
            dve.tensor_copy(keymask[:, :], keymaskf)
            dve.tensor_copy(hrows[:, :, :], hrowsf)
            dve.tensor_copy(hcols[:, :, :], hcolsf)
            for b in range(2):
                for img in range(2):
                    dve.tensor_copy(hA[b][:, :, img, 0], clsT[:, :])
            dve.memset(sc[:, 2:4], 1.0)
            dve.scalar_tensor_tensor(out=sc[:, 0:2], in0=qsc[:, :], scalar=0.25, in1=ksc[:, :],
                                     op0=ALU.mult, op1=ALU.mult).then_inc(s_const, 1)

            def stats(p, banks, full, per, st, mv, s_bn, s_ag):
                for t in range(4):
                    img, r = t // 2, ROWS[t % 2]
                    dve.wait_ge(full[img], per[img] * p + 2)
                    dve.bn_stats(st[0:r, t, :], banks[img][0:r, (t % 2) * D:(t % 2 + 1) * D]).then_inc(s_bn, 1)
                for t in range(4):
                    r = ROWS[t % 2]
                    dve.wait_ge(s_bn, 4 * p + t + 1)
                    dve.nop(nofuse=True)
                    dve.bn_aggr(mv[0:r, t, :], st[0:r, t, :]).then_inc(s_ag, 1)

            def silu_qk(p, b, c):
                bank, use = USE_A["qk", c]
                dve.wait_ge(s_th, 4 * p + c + 1)
                dve.scalar_tensor_tensor(out=s2[:, c, :], in0=th[:, c, :], scalar=1.0, in1=bankA[bank][:, 0:T2],
                                         op0=ALU.add, op1=ALU.mult).then_inc(freeA[bank], 1)

            def silu_v(p, b, t):
                bank, use = USE_A["v", t]
                r = ROWS[t % 2]
                dve.wait_ge(s_tv, 4 * p + t + 1)
                dve.scalar_tensor_tensor(out=v2[0:r, t, :], in0=tv[0:r, t, :], scalar=1.0, in1=bankA[bank][0:r, 0:D],
                                         op0=ALU.add, op1=ALU.mult).then_inc(freeA[bank], 1)

            def gate(p, b, k):
                dve.wait_ge(s_rn, 12 * p + 11)
                dve.reciprocal(r2[:, :], nwr[:, 1, :]).then_inc(s_rec, 1)

            def q_hat(p, b, c):
                bank, use = USE_A["g", c]
                dve.wait_ge(fullA[bank], N_A[bank] * p + use + 1)
                dve.scalar_tensor_tensor(out=th[:, c, :], in0=bankA[bank][:, 0:T2], scalar=1.0, in1=s2[:, c, :],
                                         op0=ALU.subtract, op1=ALU.mult).then_inc(freeA[bank], 1)

            def split_q(p, b, c):
                dve.wait_ge(s_q1, 4 * p + c + 1)
                dve.scalar_tensor_tensor(out=th[:, c, :], in0=th[:, c, :], scalar=sc[:, c:c + 1],
                                         in1=parts[0][:, c, :], op0=ALU.mult, op1=ALU.subtract).then_inc(s_r1, 1)

            def score_max(p, b, s):
                img, h = s // HEADS, s % HEADS
                at = place(h)
                if first(p):
                    dve.wait_ge(s_w, 16 * len(weights))
                dve.wait_ge(fullS, N_S * p + img * (HEADS + 1) + h + 1)
                dve.nop(nofuse=True)
                dve.tensor_tensor_reduce(out=bankS[:, 0:P], in0=bankS[:, 0:P], in1=rowmask[:, 0:P], scale=1.0,
                                         scalar=2 * NEG, op0=ALU.add, op1=ALU.max, accum_out=mx[:, img, 0, at:at + 1])
                tail = bankS[0:TAIL, P:P + TOK]
                dve.tensor_tensor_reduce(out=tail, in0=tail, in1=rowmask[0:TAIL, P:P + TOK], scale=1.0,
                                         scalar=2 * NEG, op0=ALU.add, op1=ALU.max,
                                         accum_out=mx[0:TAIL, img, 1, at:at + 1]).then_inc(freeS, 1)

            def max_out(p, b, img):
                dve.wait_ge(s_m1, 2 * p + img + 1)
                dve.tensor_tensor(mr[:, :], bankS[0:HEADS, 0:TOK], mp[:, 0, :], ALU.subtract).then_inc(freeS, 1)

            def part2(p, b, n):
                dve.wait_ge(s_p1, N_ST * p + n + 1)
                dve.tensor_tensor(p2[:, n % 2, :], p32[:, n % 2, :], p1[:, n % 2, :], ALU.subtract).then_inc(s_p2, 1)

            def heads_out(p, b, n):
                if n % 4 != 3:
                    return
                g, img = (n % HEADS) // 4, n // HEADS
                dve.wait_ge(s_pv, N_ST * p + n + 1)
                if due(8 * p):
                    dve.wait_ge(s_ot, 8 * p)
                bank, use = USE_O[n // 4]
                for c in range(2):
                    r, t = ROWS[c], 2 * img + c
                    o = bankO[bank][0:r, 4 * VW * c:4 * VW * (c + 1)].rearrange("p (h w) -> p h w", h=4)
                    dve.tensor_reduce(ot[0:r, t, 4 * g:4 * g + 4, :],
                                      o[:, :, 0:3 * HD].rearrange("p h (j d) -> p h d j", j=3), AX.X, ALU.add)
                    ins = dve.reciprocal(rd[0:r, t, 4 * g:4 * g + 4], o[:, :, 3 * HD])
                ins.then_inc(freeO[bank], 1)

            def residual(p, b, m):
                bank, use = USE_C["wo", m]
                dve.wait_ge(s_hc, 16 * (p + 1))
                if due(2 * p):
                    dve.wait_ge(s_ow, 2 * p)
                dve.wait_ge(fullC[bank], N_C[bank] * p + use + 1)
                dve.tensor_tensor(h1[:, m, :], bankC[bank][:, 0:T2], hC[:, m, :], ALU.add).then_inc(freeC[bank], 1)

            def spikes(p, b, k):
                m, j = divmod(k, STEPS + 1)
                bank, use = USE_C["ffn2", m]
                y = bankC[bank][:, 0:T2]
                if j == 0:
                    if due(16 * p):
                        dve.wait_ge(s_out, 16 * p)
                    dve.wait_ge(fullC[bank], N_C[bank] * p + use + 1)
                    dve.tensor_scalar(cn[:, m, :], y, thresholds[0], None, ALU.is_gt).then_inc(s_cn, 1)
                elif j < STEPS:
                    dve.wait_ge(s_cn, 8 * p + 4 * m + j)
                    ins = dve.scalar_tensor_tensor(out=cn[:, m, :], in0=y, scalar=thresholds[j],
                                                   in1=cn[:, m, :], op0=ALU.is_gt, op1=ALU.add)
                    ins.then_inc(s_cn if j < STEPS - 1 else freeC[bank], 1)
                else:
                    dve.wait_ge(freeC[bank], N_C[bank] * (p + 1))
                    dve.scalar_tensor_tensor(out=cn[:, m, :], in0=cn[:, m, :], scalar=1.0 / STEPS, in1=h1[:, m, :],
                                             op0=ALU.mult, op1=ALU.add).then_inc(s_ow, 1)

            run(dve, {
                "stats1": lambda p, b, k: stats(p, bankA, fullA, N_A, st1, mv1, s_bn1, s_ag1),
                "silu_qk": silu_qk, "silu_v": silu_v, "gate": gate, "q_hat": q_hat,
                "split_q": split_q, "score": score_max, "max_out": max_out, "p": part2, "o": heads_out,
                "wo_out": residual,
                "stats2": lambda p, b, k: stats(p, bankC, fullC, N_C, st2, mv2, s_bn2, s_ag2),
                "spikes": spikes})

        @block.gpsimd
        def _(pool):
            def newton(v, t, y, s, done, j):
                if due(done + j):
                    pool.wait_ge(s, done + j)
                if j == 0:
                    pool.nop(nofuse=True)
                    pool.tensor_scalar(y.bitcast(I32), v.bitcast(I32), -0.5, RSQRT_SEED, ALU.mult,
                                       ALU.add).then_inc(s, 1)
                elif j % 4 == 1:
                    pool.tensor_tensor(t, y, y, ALU.mult).then_inc(s, 1)
                elif j % 4 == 2:
                    pool.tensor_tensor(t, t, v, ALU.mult).then_inc(s, 1)
                elif j % 4 == 3:
                    pool.nop(nofuse=True)
                    pool.tensor_scalar(t, t, -0.5, 1.5, ALU.mult, ALU.add).then_inc(s, 1)
                else:
                    pool.tensor_tensor(y, y, t, ALU.mult).then_inc(s, 1)

            def rstd(p, mv, nw, s_ag, s_ln):
                pool.wait_ge(s_ag, 4 * (p + 1))
                pool.nop(nofuse=True)
                pool.tensor_scalar(nw[:, 0, :], mv[:, :, 1], LN_EPS, None, ALU.add).then_inc(s_ln, 1)
                for j in range(13):
                    newton(nw[:, 0, :], nw[:, 2, :], nw[:, 1, :], s_ln, 16 * p + 1, j)
                pool.wait_ge(s_ln, 16 * p + 14)
                pool.tensor_tensor(nw[:, 2, :], mv[:, :, 0], nw[:, 1, :], ALU.mult).then_inc(s_ln, 1)
                pool.wait_ge(s_ln, 16 * p + 15)
                pool.nop(nofuse=True)
                pool.tensor_scalar(nw[:, 2, :], nw[:, 2, :], -1.0, 0.0, ALU.mult, ALU.add).then_inc(s_ln, 1)

            def over_norm(p, b, j):
                if j == 0:
                    bank, use = USE_A["norm", 0]
                    pool.wait_ge(freeA[bank], N_A[bank] * p + use + 1)
                    pool.nop(nofuse=True)
                if j < 9:
                    newton(r2[:, :], nwr[:, 0, :], nwr[:, 1, :], s_rn, 12 * p, j)
                else:
                    pool.wait_ge(s_rn, 12 * p + j)
                    pool.nop(nofuse=True)
                    pool.tensor_scalar(nwr[:, j - 9, :], nwr[:, 1, :], NORM_EPS, float(j - 9), ALU.mult,
                                       ALU.add).then_inc(s_rn, 1)

            def gate(p, b, k):
                pool.wait_ge(s_rec, p + 1)
                pool.tensor_tensor(g_sb[:, :], nwr[:, 0, :], r2[:, :], ALU.mult).then_inc(s_rn, 1)

            def rest_v(p, b, t):
                r = ROWS[t % 2]
                pool.wait_ge(s_v1, 4 * p + t + 1)
                pool.tensor_tensor(tv[0:r, t, :].rearrange("p (h d) -> p h d", h=HEADS),
                                   v2[0:r, t, :].rearrange("p (h d) -> p h d", h=HEADS),
                                   vst[b][0:r, t, :, 0:HD], ALU.subtract).then_inc(s_rv, 1)

            def split_v(p, b, t):
                r = ROWS[t % 2]
                pool.wait_ge(s_v2, 4 * p + t + 1)
                pool.tensor_tensor(vst[b][0:r, t, :, 2 * HD:3 * HD],
                                   tv[0:r, t, :].rearrange("p (h d) -> p h d", h=HEADS),
                                   vst[b][0:r, t, :, HD:2 * HD], ALU.subtract).then_inc(s_v3, 1)

            def split_q(p, b, c):
                pool.wait_ge(s_q2, 4 * p + c + 1)
                pool.tensor_tensor(parts[2][:, c, :], th[:, c, :], parts[1][:, c, :], ALU.subtract).then_inc(s_q3, 1)

            def max_out(p, b, img):
                pool.wait_ge(s_m2, 2 * p + img + 1)
                pool.tensor_tensor(mp[:, 2, :], mr[:, :], mp[:, 1, :], ALU.subtract).then_inc(s_m3, 1)

            def heads_out(p, b, n):
                if n % 4 != 3:
                    return
                g, img = (n % HEADS) // 4, n // HEADS
                bank, use = USE_O[n // 4]
                pool.wait_ge(freeO[bank], N_O[bank] * p + use + 1)
                for c in range(2):
                    r, t = ROWS[c], 2 * img + c
                    ins = pool.tensor_tensor(ot[0:r, t, 4 * g:4 * g + 4, :], ot[0:r, t, 4 * g:4 * g + 4, :],
                                             rd[0:r, t, 4 * g:4 * g + 4].unsqueeze(2).broadcast_to([r, 4, HD]),
                                             ALU.mult)
                ins.then_inc(s_ot, 1)

            def square_relu(p, b, f):
                bank, use = USE_C["ffn1", f]
                pool.wait_ge(freeC[bank], N_C[bank] * p + use + 1)
                pool.tensor_tensor(hs[:, f, :], rr[:, f % 2, :], rr[:, f % 2, :], ALU.mult).then_inc(s_hs, 1)

            run(pool, {
                "rstd1": lambda p, b, k: rstd(p, mv1, nw1, s_ag1, s_ln1),
                "over_norm": over_norm, "gate": gate, "split_v": rest_v, "split_v2": split_v, "split_q2": split_q, "max_out2": max_out,
                "o": heads_out, "rstd2": lambda p, b, k: rstd(p, mv2, nw2, s_ag2, s_ln2),
                "ffn1_out": square_relu})


def kernel(x, cls_tok, L0_tok_W, L0_tok_b, L0_attn_Wq, L0_attn_Wk, L0_attn_Wv, L0_attn_Wo, L0_attn_q_scale,
           L0_attn_k_scale, L0_ffn_W_fc, L0_ffn_W_proj):
    import concourse.bacc as bacc
    from concourse.bass_utils import run_bass_kernel_spmd

    f = np.float32

    def features(w):
        w = np.asarray(w)
        return np.ascontiguousarray(w.T.reshape(w.shape[1] // P, P, w.shape[0]).transpose(1, 0, 2))

    n = np.asarray(x)
    patches = n.reshape(IMAGES, 3, 14, 16, 14, 16).transpose(0, 1, 2, 4, 3, 5).reshape(PAIRS, 2 * PATCHES, KC, P)
    x_t = np.ascontiguousarray(patches.transpose(0, 3, 2, 1)).reshape(PAIRS, P, KC * 2 * PATCHES)

    i, j = np.arange(P)[:, None], np.arange(P)[None, :]
    row_mask = np.zeros((P, P + TOK), f)
    row_mask[:, :P][j > i] = NEG
    row_mask[:, P:][np.arange(TOK)[None, :] > i + P] = NEG
    key_mask = np.zeros((P, P), f)
    key_mask[i > j] = NEG
    feature = np.arange(P)
    head_rows = np.zeros((P, 4, P), f)
    head_cols = np.zeros((2 * HEADS, 4, P), f)
    for c in range(4):
        head_rows[feature, c, 8 * c + feature % 8] = 1
        head_cols[8 * c + feature % 8, c, feature] = 1

    def per_feature(s):
        return np.ascontiguousarray(np.tile(np.asarray(s).reshape(DC, 8), (1, HD)).T)

    def feature_first(w):
        return np.asarray(w).reshape(DC, 8, HD, D).transpose(0, 2, 1, 3).reshape(D, D)

    arrays = {
        "x_t": x_t,
        "w_tok": features(L0_tok_W),
        "b_tok": np.ascontiguousarray(np.asarray(L0_tok_b).reshape(DC, P).T),
        "cls": np.ascontiguousarray(np.asarray(cls_tok).reshape(DC, P).T),
        "w_qk": features(np.concatenate([feature_first(L0_attn_Wq), feature_first(L0_attn_Wk)], 0)),
        "w_v": features(L0_attn_Wv),
        "w_o": features(L0_attn_Wo),
        "w_fc": features(L0_ffn_W_fc),
        "w_proj": features(L0_ffn_W_proj),
        "q_scale": per_feature(L0_attn_q_scale),
        "k_scale": per_feature(L0_attn_k_scale),
        "eye": np.eye(P, dtype=f),
        "row_mask": row_mask,
        "key_mask": key_mask,
        "head_rows": head_rows,
        "head_cols": head_cols,
    }
    nc = bacc.Bacc("TRN2", target_bir_lowering=False, num_devices=1)
    args = [nc.dram_tensor(name, a.shape, mybir.dt.from_np(a.dtype), kind="ExternalInput").ap()
            for name, a in arrays.items()]
    out_t = nc.dram_tensor("out_t", (PAIRS, P, DC * T2), F32, kind="ExternalOutput").ap()
    program(nc, *args, out_t)
    r = run_bass_kernel_spmd(nc, [arrays], core_ids=[0])
    got = r.results[0]["out_t"].reshape(PAIRS, P, DC, 2, TOK)
    return np.ascontiguousarray(got.transpose(0, 3, 4, 2, 1)).reshape(IMAGES, TOK, D)
```
